# Optimizing a Trainium2 kernel written in Bass

```python
import numpy as np
import jax
import jax.numpy as jnp

def _softmax(x, axis=-1):
    return jax.nn.softmax(x, axis=axis)

def _gelu(x):
    return jax.nn.gelu(x, approximate=True)

def _silu(x):
    return jax.nn.silu(x)

def _sigmoid(x):
    return jax.nn.sigmoid(x)

def _layernorm(x, axis=-1, eps=1e-05):
    m = jnp.mean(x, axis=axis, keepdims=True)
    v = jnp.var(x, axis=axis, keepdims=True)
    return (x - m) / jnp.sqrt(v + eps)

def _scatter_add(tgt, idx, src, axis=0):
    return tgt.at[idx].add(src)

def _segment_sum(src, seg, n):
    return jax.ops.segment_sum(src, seg, n)
kernel_name = 'mk_vit_tower_d1_tok_img256_r4_719273'

def setup_inputs(seed: int=0):
    np.random.seed(seed)
    _w = jnp.asarray

    def _rec_inputs():
        import jax
        import jax.numpy as jnp
        _rk = jax.random.key(seed)
        x = -7.10856e-05 + 0.999911 * jax.random.normal(jax.random.fold_in(_rk, 1), (64, 1, 84, 84), jnp.float32)
        return x
    x = _rec_inputs()

    def _L0_tok_setup():
        import jax, jax.numpy as jnp
        import numpy as np
        INV_SQRT2 = 0.7071067811865476

        def haar_dwt2(x):
            lo = (x[..., ::2] + x[..., 1::2]) * INV_SQRT2
            hi = (x[..., ::2] - x[..., 1::2]) * INV_SQRT2
            cA = (lo[..., ::2, :] + lo[..., 1::2, :]) * INV_SQRT2
            cH = (lo[..., ::2, :] - lo[..., 1::2, :]) * INV_SQRT2
            cV = (hi[..., ::2, :] + hi[..., 1::2, :]) * INV_SQRT2
            cD = (hi[..., ::2, :] - hi[..., 1::2, :]) * INV_SQRT2
            return (cA, (cH, cV, cD))

        def wavedec2_maps(x, levels):
            a = x
            details = []
            for _ in range(levels):
                a, d = haar_dwt2(a)
                details.append(d)
            maps = [a]
            for d in reversed(details):
                maps.extend(d)
            return maps
        key = jax.random.key(seed)
        k1, k2 = jax.random.split(key)
        B, H, W_img = (64, 256, 256)
        x = jax.random.normal(k1, (B, 1, H, W_img), dtype=jnp.float32)
        n_maps = 1 + 3 * 2
        W = jax.random.normal(k2, (n_maps, 64), dtype=jnp.float32) * (1.0 / np.sqrt(n_maps))
        b = jnp.zeros((64,), dtype=jnp.float32)
        return {'x': x, 'W': W, 'b': b}
    _L0_tok_all = _L0_tok_setup()
    _L0_tok_in = {k: v for k, v in _L0_tok_all.items() if k in ('W', 'b')}
    del _L0_tok_all

    def _L0_attn_setup():
        import jax, jax.numpy as jnp
        import numpy as np
        from math import sqrt
        DIM = 64
        key = jax.random.key(seed)
        k1, k2, k3, k4 = jax.random.split(key, 4)
        B, T, D, H, R = (2, 1024, DIM, 8, 32)

        def xavier(k, shape, fan_in, fan_out):
            a = sqrt(6.0 / (fan_in + fan_out))
            return jax.random.uniform(k, shape, jnp.float32, -a, a)
        x = jax.random.normal(k1, (B, T, D), jnp.float32)
        Q = xavier(k2, (H, R, D), D, R)
        K = xavier(k3, (H, R, D), D, R)
        VO = xavier(k4, (H, D, D), D, D)
        return {'x': x, 'Q': Q, 'K': K, 'VO': VO}
    _L0_attn_all = _L0_attn_setup()
    _L0_attn_in = {k: v for k, v in _L0_attn_all.items() if k in ('Q', 'K', 'VO')}
    del _L0_attn_all

    def _L0_ffn_setup():
        import jax, jax.numpy as jnp
        import numpy as np
        E = 8
        K = 2
        D = 64
        H = 128
        DOUT = 64
        EPS = 1e-05
        key = jax.random.key(seed)
        ks = jax.random.split(key, 9)
        s = 0.02
        return {'x': jax.random.normal(ks[0], (4, 2048, D), jnp.float32), 'gamma': 1.0 + 0.05 * jax.random.normal(ks[1], (D,), jnp.float32), 'beta': 0.05 * jax.random.normal(ks[2], (D,), jnp.float32), 'Wr': 0.01 * jax.random.normal(ks[3], (D, E), jnp.float32), 'br': jnp.zeros((E,), jnp.float32), 'W1': s * jax.random.normal(ks[4], (E, D, H), jnp.float32), 'b1': s * jax.random.normal(ks[5], (E, H), jnp.float32), 'W2': s * jax.random.normal(ks[6], (E, H, DOUT), jnp.float32), 'b2': s * jax.random.normal(ks[7], (E, DOUT), jnp.float32)}
    _L0_ffn_all = _L0_ffn_setup()
    _L0_ffn_in = {k: v for k, v in _L0_ffn_all.items() if k in ('gamma', 'beta', 'Wr', 'br', 'W1', 'b1', 'W2', 'b2')}
    del _L0_ffn_all
    return {'x': x, 'L0_tok_W': _L0_tok_in['W'], 'L0_tok_b': _L0_tok_in['b'], 'L0_attn_Q': _L0_attn_in['Q'], 'L0_attn_K': _L0_attn_in['K'], 'L0_attn_VO': _L0_attn_in['VO'], 'L0_ffn_gamma': _L0_ffn_in['gamma'], 'L0_ffn_beta': _L0_ffn_in['beta'], 'L0_ffn_Wr': _L0_ffn_in['Wr'], 'L0_ffn_br': _L0_ffn_in['br'], 'L0_ffn_W1': _L0_ffn_in['W1'], 'L0_ffn_b1': _L0_ffn_in['b1'], 'L0_ffn_W2': _L0_ffn_in['W2'], 'L0_ffn_b2': _L0_ffn_in['b2']}

def reference(x, L0_tok_W, L0_tok_b, L0_attn_Q, L0_attn_K, L0_attn_VO, L0_ffn_gamma, L0_ffn_beta, L0_ffn_Wr, L0_ffn_br, L0_ffn_W1, L0_ffn_b1, L0_ffn_W2, L0_ffn_b2):
    import jax
    import jax.numpy as jnp

    def _L0_tok_ref(x, W, b):
        import jax, jax.numpy as jnp
        import numpy as np
        INV_SQRT2 = 0.7071067811865476

        def haar_dwt2(x):
            lo = (x[..., ::2] + x[..., 1::2]) * INV_SQRT2
            hi = (x[..., ::2] - x[..., 1::2]) * INV_SQRT2
            cA = (lo[..., ::2, :] + lo[..., 1::2, :]) * INV_SQRT2
            cH = (lo[..., ::2, :] - lo[..., 1::2, :]) * INV_SQRT2
            cV = (hi[..., ::2, :] + hi[..., 1::2, :]) * INV_SQRT2
            cD = (hi[..., ::2, :] - hi[..., 1::2, :]) * INV_SQRT2
            return (cA, (cH, cV, cD))

        def wavedec2_maps(x, levels):
            a = x
            details = []
            for _ in range(levels):
                a, d = haar_dwt2(a)
                details.append(d)
            maps = [a]
            for d in reversed(details):
                maps.extend(d)
            return maps
        imgs = x[:, 0]
        B = imgs.shape[0]
        maps = wavedec2_maps(imgs, 2)
        proc = [jax.image.resize(m, (B, 8, 8), method='bilinear') for m in maps]
        feat = jnp.stack(proc, axis=1)
        feat = feat.reshape(B, feat.shape[1], 64).transpose(0, 2, 1)
        return feat @ W + b

    def _L0_attn_ref(x, Q, K, VO):
        import jax, jax.numpy as jnp
        import numpy as np
        from math import sqrt
        DIM = 64
        d = x.shape[-1]
        q = jnp.einsum('btd,hrd->bhtr', x, Q)
        k = jnp.einsum('bud,hrd->bhur', x, K)
        scores = jnp.einsum('bhtr,bhur->bhtu', q, k) / sqrt(d)
        attn = jax.nn.softmax(scores, axis=-1)
        ctx = jnp.einsum('bhtu,bud->bhtd', attn, x)
        out = jnp.einsum('bhtd,hde->bte', ctx, VO)
        return out

    def _L0_ffn_ref(x, gamma, beta, Wr, br, W1, b1, W2, b2):
        import jax, jax.numpy as jnp
        import numpy as np
        E = 8
        K = 2
        D = 64
        H = 128
        DOUT = 64
        EPS = 1e-05
        mu = jnp.mean(x, axis=-1, keepdims=True)
        var = jnp.mean(jnp.square(x - mu), axis=-1, keepdims=True)
        xn = (x - mu) * jax.lax.rsqrt(var + EPS) * gamma + beta
        logits = jnp.einsum('bsd,de->bse', xn, Wr) + br
        top_vals, top_idx = jax.lax.top_k(logits, K)
        w = jax.nn.softmax(top_vals, axis=-1)
        w_full = jnp.einsum('bsk,bske->bse', w, jax.nn.one_hot(top_idx, E, dtype=w.dtype))
        y = jnp.zeros(x.shape[:-1] + (DOUT,), x.dtype)
        for e in range(E):
            h = jax.nn.gelu(jnp.einsum('bsd,dh->bsh', xn, W1[e]) + b1[e], approximate=False)
            y_e = jnp.einsum('bsh,hd->bsd', h, W2[e]) + b2[e]
            y = y + y_e * w_full[..., e, None]
        return y
    h = _L0_tok_ref(x, L0_tok_W, L0_tok_b)
    h = h + _L0_attn_ref(_layernorm(h, axis=-1), L0_attn_Q, L0_attn_K, L0_attn_VO)
    h = h + _L0_ffn_ref(_layernorm(h, axis=-1), L0_ffn_gamma, L0_ffn_beta, L0_ffn_Wr, L0_ffn_br, L0_ffn_W1, L0_ffn_b1, L0_ffn_W2, L0_ffn_b2)
    return h

_drawn_inputs = setup_inputs


def setup_inputs(seed=0):
    import zlib

    import numpy as np

    out = dict(_drawn_inputs(seed))
    spreads = {'L0_tok_b': (0.0, 0.1), 'L0_ffn_br': (0.0, 0.539)}
    factors = {'L0_ffn_gamma': 8.0,
     'L0_ffn_beta': 8.0,
     'L0_ffn_Wr': 8.0,
     'L0_ffn_W1': 7.383,
     'L0_ffn_b1': 29.426,
     'L0_ffn_W2': 6.804,
     'L0_ffn_b2': 32.579}
    for name, (base, spread) in spreads.items():
        noise = np.random.default_rng([zlib.crc32(name.encode()), seed]).standard_normal(out[name].shape)
        drawn = base * np.exp(spread * noise) if base else spread * noise
        out[name] = jnp.asarray(drawn.astype(out[name].dtype))
    for name, factor in factors.items():
        out[name] = (out[name] * factor).astype(out[name].dtype)
    return out
```

```python
import concourse.bass as bass
from concourse import mybir
from contextlib import ExitStack

F32 = mybir.dt.float32
F32R = mybir.dt.float32r
BF16 = mybir.dt.bfloat16
ALU = mybir.AluOpType
ACT = mybir.ActivationFunctionType
AX = mybir.AxisListType

IMGS, PX, T, D = 64, 84, 64, 64
GRID = 8
HEADS, R = 8, 32
EXPERTS, HID = 8, 128
HALVES, PAIRS = 2, 16
NPAIR = HALVES * PAIRS
GP = 4
GCOL = GP * 2 * T
NG = NPAIR // GP
TOK = IMGS * T
MAPS = 7
FROWS = 64
QCOL = 512
NQ = TOK // (2 * QCOL)
EPS = 1e-5
BIG = -3.0e38


def vit_block(nc, x, tok_w, tok_b, wq, wk, wvo, gamma, beta, wr, br, w1, b1, w2, b2,
              row_ops, col_ops, ident_c, pick_c, rev_c, fold_c, out):
    ctx = ExitStack()
    with ctx:
        def sb(name, shape, dt=F32):
            return ctx.enter_context(nc.sbuf_tensor(name, shape, dt))

        def sem(name):
            return ctx.enter_context(nc.semaphore(name))

        early = sb("early", [128, IMGS * PX])
        img = early[0:PX, :].rearrange("r (b c) -> r b c", b=IMGS)
        hid = early[:, 0:4 * QCOL].rearrange("p (b c) -> p b c", b=4)
        hw = early[:, 4 * QCOL:8 * QCOL].rearrange("p (b c) -> p b c", b=4)
        yT = early[:, 8 * QCOL:9 * QCOL]
        rowop = sb("rowop", [PX, 4 * GRID])
        colop = sb("colop", [PX, 4, FROWS])
        t1 = sb("t1", [PX, 4, IMGS, GRID])
        feat = sb("feat", [FROWS + 1, IMGS * GRID])
        wtok = sb("wtok", [FROWS + 1, GRID, D])
        ident = sb("ident", [128, 128])
        identb = sb("identb", [128, 128], BF16)
        fold_f = sb("fold_f", [128, 128])
        fold = sb("fold", [128, 128], F32R)
        pick_f = sb("pick_f", [24, EXPERTS, 128])
        pick = sb("pick", [24, EXPERTS, 128], BF16)
        rev = sb("rev", [128, EXPERTS])
        h = sb("h", [128, NQ, 2, 4, D])
        xc = sb("xc", [128, NQ, 2, 4, D])
        sq = sb("sq", [128, NQ, 2, 4, D])
        x12 = sb("x12", [128, 8 * NQ, 2, D])
        xT = sb("xT", [128, TOK], F32R)
        xfT = sb("xfT", [128, TOK], F32R)
        st = sb("st", [128, 8, 8 * NQ])
        mhalf = sb("mhalf", [128, 8 * NQ])
        gam = sb("gam", [128, D])
        bet = sb("bet", [128, D])
        q_s = sb("q_s", [R, HEADS, D])
        k_s = sb("k_s", [R, HEADS, 2, D])
        qk1 = sb("qk1", [128, HEADS * D], F32R)
        qk2 = sb("qk2", [128, HEADS * D], F32R)
        vo = sb("vo", [128, 4, D])
        gq = sb("gq", [128, 2, 4, GCOL])
        xd = sb("xd", [128, 2, GCOL])
        sc = sb("sc", [128, 2, 512])
        ex = sb("ex", [128, 2, 512])
        pn = sb("pn", [128, 2, 512])
        pT = sb("pT", [128, 2, 512])
        vv = sb("vv", [128, 2, 2, 4, D])
        mx = sb("mx", [128, 2, HEADS])
        sm = sb("sm", [128, 2, HEADS])
        rs = sb("rs", [128, 2, HEADS])
        oT = sb("oT", [128, NPAIR * T])
        w1_s = sb("w1_s", [128, EXPERTS * HID])
        w1a = sb("w1a", [128, EXPERTS * HID], F32R)
        w1b = sb("w1b", [128, EXPERTS * HID], F32R)
        b1_s = sb("b1_s", [HID, EXPERTS])
        w2_s = sb("w2_s", [HID, EXPERTS, D])
        b2_s = sb("b2_s", [24, D])
        b2r = sb("b2r", [24, 2, D])
        b2p = sb("b2p", [24, 3, D], BF16)
        wr_s = sb("wr_s", [128, EXPERTS])
        wra = sb("wra", [128, EXPERTS], F32R)
        wrb = sb("wrb", [128, EXPERTS], F32R)
        br_s = sb("br_s", [128, EXPERTS])
        lg = sb("lg", [128, 8 * NQ, EXPERTS])
        lg2 = sb("lg2", [128, 8 * NQ, EXPERTS])
        oh1 = sb("oh1", [128, 8 * NQ, EXPERTS])
        oh2 = sb("oh2", [128, 8 * NQ, EXPERTS])
        ca = sb("ca", [128, 8 * NQ, EXPERTS])
        gs = sb("gs", [128, 10, 8 * NQ])
        gp = sb("gp", [128, 8 * NQ, 3, EXPERTS], BF16)
        gT = sb("gT", [24, TOK], BF16)
        gTs = sb("gTs", [24, 2 * QCOL], BF16)
        banks = ctx.enter_context(nc.psum_tensor("banks", [128, 8, 512], F32))
        ps = [banks[:, b, :] for b in range(8)]

        ld_x = [sem(f"ld_x{c}") for c in range(4)]
        ld_con, ld_tok, ld_att, ld_ffn, ld_ffp = (sem(n) for n in ("ld_con", "ld_tok", "ld_att", "ld_ffn", "ld_ffp"))
        zeroed, consts = sem("zeroed"), sem("consts")
        t1_mm, t1_sb, ft_mm, ft_sb, h_mm, h_sb = (sem(n) for n in ("t1_mm", "t1_sb", "ft_mm", "ft_sb", "h_mm", "h_sb"))
        qk_mm, qk_half, qk_sb = sem("qk_mm"), sem("qk_half"), sem("qk_sb")
        ln_v, ln_sq, ln_rs, x_split = sem("ln_v"), sem("ln_sq"), sem("ln_rs"), sem("x_split")
        xt_mm, xt_act, xt_dve = sem("xt_mm"), sem("xt_act"), sem("xt_dve")
        prep_mm, prep_sb = sem("prep_mm"), sem("prep_sb")
        s_mm, mx_done, s_sub, e_done, sm_done, r_done, p_norm = (sem(n) for n in (
            "s_mm", "mx_done", "s_sub", "e_done", "sm_done", "r_done", "p_norm"))
        t_mm, t_sb, v_mm, v_sb, o_mm, o_sb = (sem(n) for n in ("t_mm", "t_sb", "v_mm", "v_sb", "o_mm", "o_sb"))
        b_mm, b_add = sem("b_mm"), sem("b_add")
        ln2_v, ln2_sq, ln2_pw, ln2_rs, xf_split = (sem(n) for n in ("ln2_v", "ln2_sq", "ln2_pw", "ln2_rs", "xf_split"))
        xf_mm, xf_act, xf_dve = sem("xf_mm"), sem("xf_act"), sem("xf_dve")
        wsp = sem("wsp")
        lg_mm, gate_v, gate_e, gate_sp = sem("lg_mm"), sem("gate_v"), sem("gate_e"), sem("gate_sp")
        gt_mm, gt_sb, gts_sb = sem("gt_mm"), sem("gt_sb"), sem("gts_sb")
        u_mm, g_mm, hid_sb, hw_sb, y_mm, y_sb, yt_mm, h_out, stored = (sem(n) for n in (
            "u_mm", "g_mm", "hid_sb", "hw_sb", "y_mm", "y_sb", "yt_mm", "h_out", "stored"))
        block = ctx.enter_context(nc.Block())

        def heads(ap):
            return ap.rearrange("p (h u) -> p h u", u=T)

        def wide(ap):
            return ap.unsqueeze(2).to_broadcast([128, HEADS, T])

        def slots(ap):
            return ap.rearrange("p k a j e -> p (k a j) e")

        PREP, VB, TB, OB = ps[4], ps[5], ps[6], ps[7]

        FIRST = [("x", 0)] + [("g", 0, q) for q in range(4)] + [("g", 1, 0), ("g", 1, 1)]

        def units(p, g, left):
            if p == 0:
                return [(0, ("g", g + 1, 2)), (1, ("x", g + 1))] if left >= 1 else []
            if p == 1:
                return [(2, ("g", g + 1, 3))] if left >= 1 else []
            return [(p + 1, ("g", g + 2, p - 2))] if left >= 2 else []

        def attention(eng, slot):
            with eng.Fori(0, NG // 2 - 1) as i:
                for q in range(2):
                    for p in range(GP):
                        slot(i * 2 + q, q, p, i * (2 * GP) + (q * GP + p), 2)
            for q in range(2):
                for p in range(GP):
                    slot(NG - 2 + q, q, p, (NG - 2 + q) * GP + p, 1 - q)

        @block.sync
        def _(sp):
            xv = x.rearrange("b c r w -> r (b c) w")
            for c in range(4):
                sp.dma_start(img[:, c * 16:(c + 1) * 16, :], xv[:, c * 16:(c + 1) * 16, :]).then_inc(ld_x[c], 16)
            sp.dma_start(w1_s[0:D, :].rearrange("d (n k) -> d n k", k=HID), w1.rearrange("n d k -> d n k")).then_inc(ld_ffn, 16)
            sp.dma_start(w1_s[D:128, :].rearrange("d (n k) -> d n k", k=HID), w1.rearrange("n d k -> d n k")).then_inc(ld_ffn, 16)
            sp.dma_start(w2_s[:, :, :], w2.rearrange("n k d -> k n d")).then_inc(ld_ffn, 16)
            ov = out.rearrange("(f m a) (i q j) e -> f q a m i (j e)", f=HALVES, a=2, i=GRID, q=2)
            for k in range(NQ):
                sp.wait_ge(h_out, k + 1)
                for a in range(2):
                    sp.dma_start(ov[k // 2, k % 2, a], h[:, k, a, :, :].rearrange("p j e -> p (j e)")).then_inc(stored, 16)
            sp.wait_ge(stored, 32 * NQ)

        @block.gpsimd
        def _(pool):
            pool.memset(wtok[:, :, :], 0.0).then_inc(zeroed, 1)
            pool.wait_ge(zeroed, 1)
            for j in range(GRID):
                pool.dma_start(wtok[j:MAPS * GRID:GRID, j, :], tok_w).then_inc(ld_tok, 16)
            pool.dma_start(wtok[FROWS:FROWS + 1, :, :], tok_b.rearrange("(a e) -> a e", a=1).unsqueeze(1).to_broadcast([1, GRID, D])).then_inc(ld_tok, 16)
            pool.dma_start(gam[:, :], gamma.rearrange("(a e) -> a e", a=1).to_broadcast([128, D])).then_inc(ld_ffp, 16)
            pool.dma_start(bet[:, :], beta.rearrange("(a e) -> a e", a=1).to_broadcast([128, D])).then_inc(ld_ffp, 16)
            pool.dma_start(br_s[:, :], br.rearrange("(a e) -> a e", a=1).to_broadcast([128, EXPERTS])).then_inc(ld_ffp, 16)
            pool.dma_start(wr_s[0:D, :], wr).then_inc(ld_ffp, 16)
            pool.dma_start(wr_s[D:128, :], wr).then_inc(ld_ffp, 16)
            for c in range(3):
                pool.dma_start(b2_s[8 * c:8 * c + 8, :], b2).then_inc(ld_ffp, 16)
            with nc.allow_non_contiguous_dma(reason="4 KB of biases, hidden unit on partitions"):
                pool.dma_start(b1_s[:, :], b1.rearrange("n k -> k n")).then_inc(ld_ffp, 16)
            for f in range(HALVES):
                c = slice(16 * f, 16 * f + 16)
                pool.wait_ge(ln_v, 4 * f + 4)
                pool.tensor_tensor(st[:, 3, c], st[:, 2, c], mhalf[:, c], ALU.pow).then_inc(ln_rs, 1)

            def norm(n, b):
                pool.wait_ge(r_done, n + 1)
                pool.tensor_tensor(
                    pn[:, b, :].rearrange("p (q o u) -> p o q u", o=2, u=T),
                    ex[:, b, :].rearrange("p (o q u) -> p o q u", o=2, u=T),
                    rs[:, b, :].rearrange("p (o q) -> p o q", o=2).unsqueeze(3).to_broadcast([128, 2, 4, T]),
                    ALU.mult).then_inc(p_norm, 1)

            norm(0, 0)

            def slot(g, gb, p, n, left):
                if p < GP - 1 or left >= 1:
                    norm(n + 1, (p + 1) % 2)

            attention(pool, slot)
            pool.wait_ge(ln2_v, 4)
            pool.tensor_tensor(st[:, 3, :], st[:, 2, :], mhalf[:, :], ALU.pow).then_inc(ln2_pw, 1)
            pool.wait_ge(ln2_v, 6)
            pool.tensor_tensor(st[:, 5, :], st[:, 4, :], mhalf[:, :], ALU.pow).then_inc(ln2_pw, 1)

        @block.scalar
        def _(act):
            act.dma_start(rowop[:, :], row_ops).then_inc(ld_con, 16)
            act.dma_start(colop[:, :, :], col_ops).then_inc(ld_con, 16)
            act.dma_start(ident[:, :], ident_c).then_inc(ld_con, 16)
            act.dma_start(fold_f[:, :], fold_c).then_inc(ld_con, 16)
            act.dma_start(pick_f[:, :, :], pick_c).then_inc(ld_con, 16)
            act.dma_start(rev[:, :], rev_c).then_inc(ld_con, 16)
            act.dma_start(q_s[:, :, :], wq.rearrange("h r d -> r h d")).then_inc(ld_att, 16)
            for c in range(2):
                act.dma_start(k_s[:, :, c, :], wk.rearrange("h r d -> r h d")).then_inc(ld_att, 16)
            for o in range(2):
                act.dma_start(vo[64 * o:64 * o + 64, :, :], wvo.rearrange("(q o) d e -> o d q e", o=2)[o]).then_inc(ld_att, 16)
            act.wait_ge(qk_mm, 1)
            act.activation(qk1[:, :], ps[6][:, :], ACT.Copy, scale=1.0 / 8.0).then_inc(qk_half, 1)
            for c in (1, 3):
                act.wait_ge(t1_mm, c + 1)
                act.activation(t1[:, :, 16 * c:16 * c + 16, :].rearrange("c r b i -> c b r i"),
                               ps[c][0:PX, :].rearrange("c (b r i) -> c b r i", b=16, r=4), ACT.Copy).then_inc(t1_sb, 1)
            for m in (1, 3):
                act.wait_ge(h_mm, m + 1)
                act.activation(h[:, m - 1:m + 1, 1, :, :], ps[m][:, :].rearrange("p (q j e) -> p q j e", q=2, e=D),
                               ACT.Copy).then_inc(h_sb, 1)
            for f in range(HALVES):
                act.wait_ge(ln_v, 4 * f + 2)
                act.activation(sq[:, 2 * f:2 * f + 2], xc[:, 2 * f:2 * f + 2], ACT.Square).then_inc(ln_sq, 1)
            for c in (1, 3, 5, 7):
                act.wait_ge(xt_mm, c + 1)
                f, q, a = c // 4, (c // 2) % 2, c % 2
                act.activation(
                    xT[:, :].rearrange("p (f m a j i) -> p f a j m i", f=2, m=PAIRS, a=2, i=GRID)[:, f, a, 4 * q:4 * q + 4],
                    ps[c % 4][:, :].rearrange("p (j m i) -> p j m i", j=4, i=GRID), ACT.Copy).then_inc(xt_act, 1)

            count = {"prep": 0}

            def prep(k, u):
                act.wait_ge(prep_mm, k + 1)
                if u[0] == "x":
                    act.activation(xd[:, u[2], :], PREP[:, :], ACT.Copy).then_inc(prep_sb, 1)
                else:
                    act.activation(gq[:, u[2], u[3], :], PREP[:, :], ACT.Copy).then_inc(prep_sb, 1)

            def with_buffer(u, gb):
                return (u[0], u[1], gb) + tuple(u[2:])

            def exps(n, b):
                act.wait_ge(s_sub, n + 1)
                act.activation(ex[:, b, :], sc[:, b, :], ACT.Exp).then_inc(e_done, 1)

            def v_evac(n, b):
                act.wait_ge(v_mm, n + 1)
                act.activation(vv[:, b].rearrange("p a q e -> p (a q e)"), VB[:, :], ACT.Copy).then_inc(v_sb, 1)

            for k, u in enumerate(FIRST):
                prep(k, with_buffer(u, u[1] % 2))
            exps(0, 0)
            v_evac(0, 0)
            exps(1, 1)

            def slot(g, gb, p, n, left):
                act.wait_ge(t_mm, n + 1)
                act.activation(pT[:, p % 2, :], TB[:, :], ACT.Copy).then_inc(t_sb, 1)
                for k, u in units(p, 0, left):
                    prep(g * 5 + (len(FIRST) + k), with_buffer(u, (gb + u[1]) % 2))
                if p < 3 or left >= 1:
                    v_evac(n + 1, (p + 1) % 2)
                if p < 2 or left >= 1:
                    exps(n + 2, p % 2)
                if p == GP - 1:
                    act.wait_ge(o_mm, g + 1)
                    act.activation(oT[:, :].rearrange("p (j c) -> p j c", j=GRID)[:, :, bass.ds(g * (GP * GRID), GP * GRID)].rearrange("p j (m i) -> p j m i", i=GRID),
                                   OB[:, 0:GP * T].rearrange("p (m j i) -> p j m i", m=GP, j=GRID), ACT.Copy).then_inc(o_sb, 1)

            attention(act, slot)
            act.wait_ge(ln2_v, 2)
            act.activation(slots(sq[:]), slots(xc[:]), ACT.Square).then_inc(ln2_sq, 1)
            for c in (1, 3, 5, 7):
                act.wait_ge(xf_mm, c + 1)
                act.activation(xfT[:, c * 512:(c + 1) * 512], ps[c % 4][:, :], ACT.Copy).then_inc(xf_act, 1)
            act.wait_ge(gate_v, 13)
            act.activation(gs[:, 5, :], gs[:, 4, :], ACT.Exp).then_inc(gate_e, 1)
            with act.Fori(0, NQ) as k:
                for n in range(EXPERTS):
                    for a in range(2):
                        b = 2 * (n % 2) + a
                        act.wait_ge(u_mm, k * 16 + (2 * n + a + 1))
                        act.activation(hid[:, b, :], ps[b][:, :], ACT.Gelu, bias=b1_s[:, n:n + 1]).then_inc(hid_sb, 1)
                act.wait_ge(y_mm, k * 8 + 8)
                act.activation(yT[:, :], ps[6][:, :], ACT.Copy).then_inc(y_sb, 1)

        @block.vector
        def _(dve):
            dve.memset(feat[FROWS:FROWS + 1, :], 1.0)
            dve.memset(mhalf[:, :], -0.5)
            dve.wait_ge(ld_con, 96)
            dve.tensor_copy(identb[:, :], ident[:, :]).then_inc(consts, 1)
            dve.tensor_copy(fold[:, :], fold_f[:, :]).then_inc(consts, 1)
            dve.tensor_copy(pick[:, :, :], pick_f[:, :, :]).then_inc(consts, 1)
            dve.wait_ge(qk_half, 1)
            dve.scalar_tensor_tensor(qk2[:, :], ps[6][:, :], 1.0 / 8.0, qk1[:, :].bitcast(F32),
                                     op0=ALU.mult, op1=ALU.subtract).then_inc(qk_sb, 1)
            for c in (0, 2):
                dve.wait_ge(t1_mm, c + 1)
                dve.tensor_copy(t1[:, :, 16 * c:16 * c + 16, :].rearrange("c r b i -> c b r i"),
                                ps[c][0:PX, :].rearrange("c (b r i) -> c b r i", b=16, r=4)).then_inc(t1_sb, 1)
            dve.wait_ge(ft_mm, 1)
            for f in range(HALVES):
                dve.tensor_copy(feat[0:FROWS, 256 * f:256 * f + 256].rearrange("k (a m i) -> k a m i", a=2, i=GRID),
                                ps[4][0:FROWS, 256 * f:256 * f + 256].rearrange("k (m a i) -> k a m i", a=2, i=GRID)).then_inc(ft_sb, 1)
            for m in (0, 2):
                dve.wait_ge(h_mm, m + 1)
                dve.tensor_copy(h[:, m:m + 2, 0, :, :], ps[m][:, :].rearrange("p (q j e) -> p q j e", q=2, e=D)).then_inc(h_sb, 1)

            def half_slots(t, f):
                return t[:, 2 * f:2 * f + 2].rearrange("p k a j e -> p (k a j) e")

            def bcast(ap, n=16):
                return ap.unsqueeze(2).to_broadcast([128, n, D])

            for f in range(HALVES):
                c = slice(16 * f, 16 * f + 16)
                v = 4 * f
                dve.wait_ge(h_sb, 4)
                dve.reduce_sum(st[:, 0, c], half_slots(h, f), axis=AX.X).then_inc(ln_v, 1)
                dve.wait_ge(ln_v, v + 1)
                dve.scalar_tensor_tensor(half_slots(xc, f), bcast(st[:, 0, c]), -1.0 / D, half_slots(h, f),
                                         op0=ALU.mult, op1=ALU.add).then_inc(ln_v, 1)
                dve.wait_ge(ln_sq, f + 1)
                dve.reduce_sum(st[:, 1, c], half_slots(sq, f), axis=AX.X).then_inc(ln_v, 1)
                dve.wait_ge(ln_v, v + 3)
                dve.tensor_scalar(st[:, 2, c], st[:, 1, c], 1.0 / D, EPS, ALU.mult, ALU.add).then_inc(ln_v, 1)
                dve.wait_ge(ln_rs, f + 1)
                dve.tensor_tensor(half_slots(sq, f), half_slots(xc, f), bcast(st[:, 3, c]), ALU.mult).then_inc(x_split, 1)
                dve.wait_ge(x_split, 3 * f + 1)
                dve.tensor_copy(x12[:, c, 0, :].bitcast(F32R), half_slots(sq, f)).then_inc(x_split, 1)
                dve.wait_ge(x_split, 3 * f + 2)
                dve.tensor_tensor(x12[:, c, 1, :], half_slots(sq, f), x12[:, c, 0, :], ALU.subtract).then_inc(x_split, 1)
            for c in (0, 2, 4, 6):
                dve.wait_ge(xt_mm, c + 1)
                f, q, a = c // 4, (c // 2) % 2, c % 2
                dve.tensor_copy(
                    xT[:, :].rearrange("p (f m a j i) -> p f a j m i", f=2, m=PAIRS, a=2, i=GRID)[:, f, a, 4 * q:4 * q + 4],
                    ps[c % 4][:, :].rearrange("p (j m i) -> p j m i", j=4, i=GRID)).then_inc(xt_dve, 1)

            def less_max(n, b):
                dve.wait_ge(s_mm, n + 1)
                raw = banks[:, 2 * b:2 * b + 2, 0:256].rearrange("p o (q u) -> p o q u", u=T)
                peak = mx[:, b, :].rearrange("p (o q) -> p o q", o=2)
                dve.reduce_max(peak, raw, axis=AX.X).then_inc(mx_done, 1)
                dve.wait_ge(mx_done, n + 1)
                dve.tensor_tensor(sc[:, b, :].rearrange("p (o q u) -> p o q u", o=2, u=T), raw,
                                  peak.unsqueeze(3).to_broadcast([128, 2, 4, T]), ALU.subtract).then_inc(s_sub, 1)

            def sums(n, b):
                dve.wait_ge(e_done, n + 1)
                dve.reduce_sum(sm[:, b, :], heads(ex[:, b, :]), axis=AX.X).then_inc(sm_done, 1)
                dve.wait_ge(sm_done, n + 1)
                dve.reciprocal(rs[:, b, :], sm[:, b, :]).then_inc(r_done, 1)

            less_max(0, 0)
            sums(0, 0)
            less_max(1, 1)

            def slot(g, gb, p, n, left):
                if p < 3 or left >= 1:
                    sums(n + 1, (p + 1) % 2)
                if p < 2 or left >= 1:
                    less_max(n + 2, p % 2)

            attention(dve, slot)
            for c in range(4):
                dve.wait_ge(b_mm, c + 1)
                dve.tensor_tensor(h[:, c].rearrange("p a j e -> p j a e"), h[:, c].rearrange("p a j e -> p j a e"),
                                  ps[c][:, :].rearrange("p (j a e) -> p j a e", j=4, e=D), ALU.add).then_inc(b_add, 1)
            dve.wait_ge(b_add, 4)
            dve.reduce_sum(st[:, 0, :], slots(h[:]), axis=AX.X).then_inc(ln2_v, 1)
            dve.wait_ge(ln2_v, 1)
            dve.scalar_tensor_tensor(slots(xc[:]), bcast(st[:, 0, :], 32), -1.0 / D, slots(h[:]),
                                     op0=ALU.mult, op1=ALU.add).then_inc(ln2_v, 1)
            dve.wait_ge(ln2_sq, 1)
            dve.reduce_sum(st[:, 1, :], slots(sq[:]), axis=AX.X).then_inc(ln2_v, 1)
            dve.wait_ge(ln2_v, 3)
            dve.tensor_scalar(st[:, 2, :], st[:, 1, :], 1.0 / D, EPS, ALU.mult, ALU.add).then_inc(ln2_v, 1)
            dve.wait_ge(ln2_pw, 1)
            dve.tensor_tensor(st[:, 6, :], st[:, 3, :], st[:, 3, :], ALU.mult).then_inc(ln2_v, 1)
            dve.wait_ge(ln2_v, 5)
            dve.tensor_scalar(st[:, 4, :], st[:, 6, :], -EPS, 1.0 + EPS, ALU.mult, ALU.add).then_inc(ln2_v, 1)
            dve.wait_ge(ln2_pw, 2)
            dve.tensor_tensor(st[:, 7, :], st[:, 5, :], st[:, 3, :], ALU.mult).then_inc(ln2_rs, 1)
            dve.wait_ge(ln2_rs, 1)
            dve.wait_ge(ld_ffn, 16 * 3)
            dve.wait_ge(ld_ffp, 16 * 9)
            dve.tensor_tensor(slots(sq[:]), slots(xc[:]), bcast(st[:, 7, :], 32), ALU.mult).then_inc(ln2_rs, 1)
            dve.wait_ge(ln2_rs, 2)
            dve.tensor_tensor(slots(xc[:]), slots(sq[:]), gam[:, :].unsqueeze(1).to_broadcast([128, 32, D]), ALU.mult).then_inc(ln2_rs, 1)
            dve.wait_ge(ln2_rs, 3)
            dve.tensor_tensor(slots(sq[:]), slots(xc[:]), bet[:, :].unsqueeze(1).to_broadcast([128, 32, D]), ALU.add).then_inc(ln2_rs, 1)
            dve.wait_ge(ln2_rs, 4)
            dve.tensor_copy(x12[:, :, 0, :].bitcast(F32R), slots(sq[:])).then_inc(xf_split, 1)
            dve.wait_ge(xf_split, 1)
            dve.tensor_tensor(x12[:, :, 1, :], slots(sq[:]), x12[:, :, 0, :], ALU.subtract).then_inc(xf_split, 1)
            dve.tensor_copy(w1a[:, :], w1_s[:, :]).then_inc(wsp, 1)
            dve.tensor_copy(wra[:, :], wr_s[:, :]).then_inc(wsp, 1)
            dve.tensor_copy(b2p[:, 0, :], b2_s[:, :]).then_inc(wsp, 1)
            dve.wait_ge(wsp, 3)
            dve.tensor_tensor(w1b[:, :], w1_s[:, :], w1a[:, :].bitcast(F32), ALU.subtract).then_inc(wsp, 1)
            dve.tensor_tensor(wrb[:, :], wr_s[:, :], wra[:, :].bitcast(F32), ALU.subtract).then_inc(wsp, 1)
            dve.tensor_tensor(b2r[:, 0, :], b2_s[:, :], b2p[:, 0, :], ALU.subtract).then_inc(wsp, 1)
            dve.wait_ge(wsp, 6)
            dve.tensor_copy(b2p[:, 1, :], b2r[:, 0, :]).then_inc(wsp, 1)
            dve.wait_ge(wsp, 7)
            dve.tensor_tensor(b2p[:, 2, :], b2r[:, 0, :], b2p[:, 1, :], ALU.subtract).then_inc(wsp, 1)
            for c in (0, 2, 4, 6):
                dve.wait_ge(xf_mm, c + 1)
                dve.tensor_copy(xfT[:, c * 512:(c + 1) * 512], ps[c % 4][:, :]).then_inc(xf_dve, 1)
            E32 = [128, 8 * NQ, EXPERTS]
            up = lambda ap: ap.unsqueeze(2).to_broadcast(E32)
            across = lambda ap: ap.unsqueeze(1).to_broadcast(E32)
            g = [0]

            def link(ins):
                g[0] += 1
                ins.then_inc(gate_v, 1)
                dve.wait_ge(gate_v, g[0])

            dve.wait_ge(lg_mm, 1)
            link(dve.tensor_tensor(lg[:, :, :], ps[4][:, 0:256].rearrange("p (s n) -> p s n", n=EXPERTS), across(br_s[:, :]), ALU.add))

            def first_largest(src, onehot, m, at):
                link(dve.reduce_max(gs[:, m, :], src[:, :, :], axis=AX.X))
                link(dve.tensor_tensor(onehot[:, :, :], src[:, :, :], up(gs[:, m, :]), ALU.is_equal))
                link(dve.tensor_tensor(ca[:, :, :], onehot[:, :, :], across(rev[:, :]), ALU.mult))
                link(dve.reduce_max(gs[:, at, :], ca[:, :, :], axis=AX.X))
                link(dve.tensor_tensor(onehot[:, :, :], ca[:, :, :], up(gs[:, at, :]), ALU.is_equal))

            first_largest(lg, oh1, 0, 1)
            link(dve.scalar_tensor_tensor(lg2[:, :, :], oh1[:, :, :], BIG, lg[:, :, :], op0=ALU.mult, op1=ALU.add))
            first_largest(lg2, oh2, 2, 3)
            link(dve.tensor_tensor(gs[:, 4, :], gs[:, 2, :], gs[:, 0, :], ALU.subtract))
            dve.wait_ge(gate_e, 1)
            link(dve.tensor_scalar(gs[:, 6, :], gs[:, 5, :], 1.0, None, ALU.add))
            link(dve.reciprocal(gs[:, 7, :], gs[:, 6, :]))
            link(dve.tensor_tensor(gs[:, 8, :], gs[:, 5, :], gs[:, 7, :], ALU.mult))
            link(dve.tensor_tensor(lg[:, :, :], oh1[:, :, :], up(gs[:, 7, :]), ALU.mult))
            link(dve.tensor_tensor(lg2[:, :, :], oh2[:, :, :], up(gs[:, 8, :]), ALU.mult))
            link(dve.tensor_tensor(ca[:, :, :], lg[:, :, :], lg2[:, :, :], ALU.add))
            link(dve.tensor_copy(gp[:, :, 0, :], ca[:, :, :]))
            link(dve.tensor_tensor(lg[:, :, :], ca[:, :, :], gp[:, :, 0, :], ALU.subtract))
            link(dve.tensor_copy(gp[:, :, 1, :], lg[:, :, :]))
            dve.tensor_tensor(gp[:, :, 2, :], lg[:, :, :], gp[:, :, 1, :], ALU.subtract).then_inc(gate_sp, 1)
            for c in range(4):
                dve.wait_ge(gt_mm, c + 1)
                dve.tensor_copy(gT[:, c * 1024:(c + 1) * 1024], ps[c][0:24, :].bitcast(BF16)).then_inc(gt_sb, 1)
            dve.wait_ge(gt_sb, 4)
            with dve.Fori(0, NQ) as k:
                dve.tensor_copy(gTs[:, :], gT[:, bass.ds(k * (2 * QCOL), 2 * QCOL)]).then_inc(gts_sb, 1)
                for n in range(EXPERTS):
                    for a in range(2):
                        b = 2 * (n % 2) + a
                        dve.wait_ge(hid_sb, k * 16 + (2 * n + a + 1))
                        dve.wait_ge(g_mm, k * 16 + (2 * n + a + 1))
                        if n >= 2:
                            dve.wait_ge(y_mm, k * 8 + (n - 1))
                        dve.tensor_tensor(hw[:, b, :], hid[:, b, :], ps[4 + a][:, :], ALU.mult).then_inc(hw_sb, 1)
                dve.wait_ge(yt_mm, k + 1)
                hk = h[:, :, :, :, :].rearrange("p k a j e -> p (k a j e)")[:, bass.ds(k * 512, 512)].rearrange("p (a j e) -> p j a e", a=2, e=D)
                dve.tensor_tensor(hk, hk, ps[7][:, :].rearrange("p (j a e) -> p j a e", j=4, e=D), ALU.add).then_inc(h_out, 1)

        @block.tensor
        def _(pe):
            pe.wait_ge(ld_att, 80)
            for hd in range(HEADS):
                last = pe.matmul(ps[6][:, hd * D:(hd + 1) * D], k_s[:, hd, :, :], q_s[:, hd, :], start=True, stop=True)
            last.then_inc(qk_mm, 1)
            pe.wait_ge(ld_con, 96)
            for c in range(4):
                pe.wait_ge(ld_x[c], 16)
                for b in range(16):
                    last = pe.matmul(ps[c][0:PX, 32 * b:32 * b + 32], img[:, 16 * c + b, :], rowop[:, :], start=True, stop=True)
                last.then_inc(t1_mm, 1)
            pe.wait_ge(t1_sb, 4)
            for r in range(4):
                last = pe.matmul(ps[4][0:FROWS, :], colop[:, r, :], t1[:, r, :, :].rearrange("c b i -> c (b i)"), start=r == 0, stop=r == 3)
            last.then_inc(ft_mm, 1)
            pe.wait_ge(ft_sb, 2)
            pe.wait_ge(ld_tok, 16 * 9)
            for m in range(4):
                pe.matmul(ps[m][:, :], feat[:, 128 * m:128 * m + 128], wtok[:, :, :].rearrange("k j e -> k (j e)"), start=True, stop=True).then_inc(h_mm, 1)
            for c in range(8):
                if c % 4 == 0:
                    pe.wait_ge(x_split, 3 * (c // 4) + 3)
                if c >= 4:
                    pe.wait_ge((xt_act, xt_dve)[(c + 1) % 2], (c - 4) // 2 + 1)
                if c % 4 == 0:
                    pe.wait_ge(h_sb, 4)
                for j in range(4):
                    last = pe.transpose(ps[c % 4][:, 128 * j:128 * j + 128], x12[:, 4 * c + j, :, :].rearrange("p a e -> p (a e)"), ident[:, :])
                last.then_inc(xt_mm, 1)
            pe.wait_ge(xt_act, 4)
            pe.wait_ge(xt_dve, 4)
            pe.wait_ge(consts, 3)
            pe.wait_ge(qk_sb, 1)

            def prep(k, u, g):
                if not (isinstance(k, int) and k == 0):
                    pe.wait_ge(prep_sb, k)
                cols = xT[:, bass.ds(g * GCOL, GCOL)]
                if u[0] == "x":
                    pe.matmul(PREP[:, :], fold[:, :], cols, start=True, stop=True).then_inc(prep_mm, 1)
                else:
                    w = slice(128 * u[2], 128 * u[2] + 128)
                    pe.matmul(PREP[:, :], qk1[:, w], cols, start=True, stop=False)
                    pe.matmul(PREP[:, :], qk2[:, w], cols, start=False, stop=True).then_inc(prep_mm, 1)

            def scores(n, gb, p, b):
                for c in ((0, 0), (1, 1), (1, 0), (0, 1)):
                    o, a = c
                    t0 = 128 * p + 64 * a
                    last = pe.matmul(banks[64 * a:64 * a + 64, 2 * b + o, 0:256], xd[64 * o:64 * o + 64, gb, t0:t0 + 64],
                                     gq[64 * o:64 * o + 64, gb, :, t0:t0 + 64], start=True, stop=True)
                last.then_inc(s_mm, 1)

            def values(n, gb, p):
                for a in range(2):
                    for o in range(2):
                        t0 = 128 * p + 64 * a
                        last = pe.matmul(VB[64 * o:64 * o + 64, 256 * a:256 * a + 256], xd[64 * o:64 * o + 64, gb, t0:t0 + 64],
                                         vo[64 * o:64 * o + 64, :, :].rearrange("p q e -> p (q e)"), start=True, stop=True)
                last.then_inc(v_mm, 1)

            for k, u in enumerate(FIRST):
                prep(k, u, u[1])
            pe.wait_ge(prep_sb, 5)
            scores(0, 0, 0, 0)
            values(0, 0, 0)
            scores(1, 0, 1, 1)

            def slot(g, gb, p, n, left):
                pe.wait_ge(v_sb, n + 1)
                pe.wait_ge(p_norm, n + 1)
                for q in range(4):
                    last = pe.transpose(TB[:, 128 * q:128 * q + 128], pn[:, p % 2, 128 * q:128 * q + 128], ident[:, :])
                last.then_inc(t_mm, 1)
                if p == 0 or p == 1:
                    scores(n + 2, gb, p + 2, p % 2)
                if p == 2 and left == 1:
                    pe.wait_ge(prep_sb, g * 5 + 10)
                for k, u in units(p, 0, left):
                    prep(g * 5 + (len(FIRST) + k), u, g + u[1])
                if p >= 2 and left >= 1:
                    scores(n + 2, 1 - gb, p - 2, p % 2)
                if p < 3:
                    values(n + 1, gb, p + 1)
                elif left >= 1:
                    values(n + 1, 1 - gb, 0)
                pe.wait_ge(t_sb, n + 1)
                for q in range(4):
                    for a in range(2):
                        last = pe.matmul(OB[64 * a:64 * a + 64, T * p:T * p + T], vv[:, p % 2, a, q, :],
                                         pT[:, p % 2, 128 * q + 64 * a:128 * q + 64 * a + 64], start=q == 0, stop=q == 3)
                if p == GP - 1:
                    last.then_inc(o_mm, 1)

            attention(pe, slot)
            pe.wait_ge(o_sb, NG)
            ov = oT[:, :].rearrange("p (j f c) -> p f j c", j=GRID, f=HALVES)
            for c in range(4):
                for j in range(4):
                    last = pe.transpose(ps[c][:, 128 * j:128 * j + 128], ov[:, c // 2, 4 * (c % 2) + j], ident[:, :])
                last.then_inc(b_mm, 1)
            pe.wait_ge(xf_split, 2)
            for c in range(8):
                if c >= 4:
                    pe.wait_ge((xf_act, xf_dve)[(c + 1) % 2], (c - 4) // 2 + 1)
                for j in range(4):
                    last = pe.transpose(ps[c % 4][:, 128 * j:128 * j + 128], x12[:, 4 * c + j, :, :].rearrange("p a e -> p (a e)"), ident[:, :])
                last.then_inc(xf_mm, 1)
            pe.wait_ge(wsp, 8)
            pe.wait_ge(xf_act, 4)
            pe.wait_ge(xf_dve, 4)
            for s in range(8 * NQ):
                pe.matmul(ps[4][:, 8 * s:8 * s + 8], xfT[:, 128 * s:128 * s + 128], wra[:, :], start=True, stop=False)
                last = pe.matmul(ps[4][:, 8 * s:8 * s + 8], xfT[:, 128 * s:128 * s + 128], wrb[:, :], start=False, stop=True)
            last.then_inc(lg_mm, 1)
            pe.wait_ge(gate_sp, 1)
            for c in range(4):
                for s in range(8):
                    last = pe.transpose(ps[c][0:24, :].bitcast(BF16)[:, 128 * s:128 * s + 128],
                                        gp[:, 8 * c + s, :, :].rearrange("p c n -> p (c n)"), identb[:, :])
                last.then_inc(gt_mm, 1)
            pe.wait_ge(gt_sb, 4)

            with pe.Fori(0, NQ) as k:
                pe.wait_ge(gts_sb, k + 1)

                def hidden(n):
                    for a in range(2):
                        b = 2 * (n % 2) + a
                        if n >= 2:
                            pe.wait_ge(hid_sb, k * 16 + (2 * (n - 2) + a + 1))
                        cols = xfT[:, bass.ds(k * (2 * QCOL) + a * QCOL, QCOL)]
                        pe.matmul(ps[b][:, :], w1a[:, n * HID:(n + 1) * HID], cols, start=True, stop=False)
                        pe.matmul(ps[b][:, :], w1b[:, n * HID:(n + 1) * HID], cols, start=False, stop=True).then_inc(u_mm, 1)

                def spread(n):
                    for a in range(2):
                        if n >= 1:
                            pe.wait_ge(hw_sb, k * 16 + (2 * (n - 1) + a + 1))
                        pe.matmul(ps[4 + a][:, :], pick[:, n, :], gTs[:, a * QCOL:(a + 1) * QCOL], start=True, stop=True).then_inc(g_mm, 1)

                hidden(0)
                spread(0)
                for c in range(3):
                    for a in range(2):
                        pe.matmul(ps[6][64 * a:64 * a + 64, :], b2p[:, c, :], gTs[:, a * QCOL:(a + 1) * QCOL],
                                  start=c == 0, stop=False)
                for n in range(EXPERTS):
                    if n + 1 < EXPERTS:
                        hidden(n + 1)
                        spread(n + 1)
                    pe.wait_ge(hw_sb, k * 16 + (2 * n + 2))
                    for a in range(2):
                        last = pe.matmul(ps[6][64 * a:64 * a + 64, :], w2_s[:, n, :], hw[:, 2 * (n % 2) + a, :],
                                         start=False, stop=n == EXPERTS - 1)
                    last.then_inc(y_mm, 1)
                pe.wait_ge(y_sb, k + 1)
                for j in range(4):
                    last = pe.transpose(ps[7][:, 128 * j:128 * j + 128], yT[:, 128 * j:128 * j + 128], ident[:, :])
                last.then_inc(yt_mm, 1)


def _half_size(n):
    import numpy as np
    lo, hi = np.zeros((n // 2, n)), np.zeros((n // 2, n))
    for i in range(n // 2):
        lo[i, 2 * i] = lo[i, 2 * i + 1] = hi[i, 2 * i] = 0.7071067811865476
        hi[i, 2 * i + 1] = -0.7071067811865476
    return lo, hi


def _resize(n, m):
    import numpy as np
    at = (np.arange(m) + 0.5) * n / m - 0.5
    w = np.maximum(0.0, 1.0 - np.abs(at[:, None] - np.arange(n)[None]) * m / n)
    return w / w.sum(1, keepdims=True)


def _constants():
    import numpy as np
    lo1, hi1 = _half_size(PX)
    lo2, hi2 = _half_size(PX // 2)
    small, large = _resize(PX // 4, GRID), _resize(PX // 2, GRID)
    ops = [small @ lo2 @ lo1, small @ hi2 @ lo1, large @ lo1, large @ hi1]
    rows = np.concatenate(ops, 0).T
    maps = [(0, 0), (1, 0), (0, 1), (1, 1), (3, 2), (2, 3), (3, 3)]
    cols = np.zeros((PX, 4, FROWS))
    for m, (r, c) in enumerate(maps):
        cols[:, r, m * GRID:(m + 1) * GRID] = ops[c].T
    ident = np.eye(128)
    pick = np.zeros((24, EXPERTS, 128))
    for e in range(EXPERTS):
        pick[e::EXPERTS, e, :] = 1.0
    rev = np.tile(EXPERTS - np.arange(EXPERTS), (128, 1))
    fold = np.tile(np.eye(D), (2, 2))
    return [np.ascontiguousarray(a, dtype=np.float32) for a in (rows, cols, ident, pick, rev, fold)]


_INS = ['x', 'L0_tok_W', 'L0_tok_b', 'L0_attn_Q', 'L0_attn_K', 'L0_attn_VO', 'L0_ffn_gamma', 'L0_ffn_beta', 'L0_ffn_Wr',
        'L0_ffn_br', 'L0_ffn_W1', 'L0_ffn_b1', 'L0_ffn_W2', 'L0_ffn_b2']
_CONST = ['row_ops', 'col_ops', 'ident', 'pick', 'rev', 'fold']


def kernel(**inputs):
    import numpy as _np
    import concourse.bacc as _bacc
    from concourse import mybir as _mybir
    from concourse.bass_utils import run_bass_kernel_spmd as _run

    nc = _bacc.Bacc("TRN2", target_bir_lowering=False, num_devices=1)
    arrays, args = {}, []
    given = [(n, _np.ascontiguousarray(inputs[n])) for n in _INS] + list(zip(_CONST, _constants()))
    for name, a in given:
        arrays[f"in_{name}_dram"] = a
        args.append(nc.dram_tensor(f"in_{name}_dram", a.shape, _mybir.dt.from_np(a.dtype), kind="ExternalInput").ap())
    args.append(nc.dram_tensor("out_dram", (IMGS, T, D), _mybir.dt.float32, kind="ExternalOutput").ap())
    vit_block(nc, *args)
    r = _run(nc, [arrays], core_ids=[0])
    return r.results[0]["out_dram"]
```

```python
import concourse.bass as bass
from concourse import mybir
from contextlib import ExitStack

F32 = mybir.dt.float32
F32R = mybir.dt.float32r
BF16 = mybir.dt.bfloat16
ALU = mybir.AluOpType
ACT = mybir.ActivationFunctionType
AX = mybir.AxisListType

IMGS, PX, T, D = 64, 84, 64, 64
GRID = 8
HEADS, R = 8, 32
EXPERTS, HID = 8, 128
HALVES, PAIRS = 2, 16
NPAIR = HALVES * PAIRS
GP = 4
GCOL = GP * 2 * T
NG = NPAIR // GP
TOK = IMGS * T
MAPS = 7
FROWS = 64
QCOL = 512
NQ = TOK // (2 * QCOL)
EPS = 1e-5
BIG = -3.0e38
MAGIC = 0x5F3759DF
I32 = mybir.dt.int32
SIDE_USES = 9


def vit_block(nc, x, tok_w, tok_b, wq, wk, wvo, gamma, beta, wr, br, w1, b1, w2, b2,
              row_ops, col_ops, ident_c, pick_c, rev_c, fold_c, mask_c, one_c, out):
    ctx = ExitStack()
    with ctx:
        def sb(name, shape, dt=F32):
            return ctx.enter_context(nc.sbuf_tensor(name, shape, dt))

        def sem(name):
            return ctx.enter_context(nc.semaphore(name))

        early = sb("early", [128, IMGS * PX])
        img = early[0:PX, :].rearrange("r (b c) -> r b c", b=IMGS)
        hid = early[:, 0:4 * QCOL].rearrange("p (b c) -> p b c", b=4)
        hw = early[:, 4 * QCOL:8 * QCOL].rearrange("p (b c) -> p b c", b=4)
        yT = early[:, 8 * QCOL:9 * QCOL]
        rowop = sb("rowop", [PX, 4 * GRID])
        colop = sb("colop", [PX, 4, FROWS])
        t0 = sb("t0", [128, PAIRS, PX])
        t1 = sb("t1", [PX, 16, PAIRS, GRID])
        feat = sb("feat", [128, 2 * PAIRS * GRID])
        one = sb("one", [128, 1])
        mask = sb("mask", [128, GRID])
        wrep = sb("wrep", [128, D])
        wavg = sb("wavg", [128, 1])
        wtok = sb("wtok", [128, GRID, D])
        wmean = sb("wmean", [128, GRID])
        ident = sb("ident", [128, 128])
        identb = sb("identb", [128, 128], BF16)
        fold_f = sb("fold_f", [128, 128])
        fold = sb("fold", [128, 128], F32R)
        pick_f = sb("pick_f", [24, EXPERTS, 128])
        pick = sb("pick", [24, EXPERTS, 128], BF16)
        rev = sb("rev", [128, EXPERTS])
        h = sb("h", [128, NQ, 2, 4, D])
        xc = sb("xc", [128, NQ, 2, 4, D])
        sq = sb("sq", [128, NQ, 2, 4, D])
        x12 = sb("x12", [128, 8 * NQ, 2, D])
        xT = sb("xT", [128, TOK], F32R)
        xfT = sb("xfT", [128, TOK], F32R)
        mean = sb("mean", [128, 8 * NQ])
        var = sb("var", [128, 8 * NQ])
        hvar = sb("hvar", [128, 8 * NQ])
        rstd = sb("rstd", [128, 8 * NQ])
        tmp = sb("tmp", [128, 8 * NQ])
        gam = sb("gam", [128, 1])
        bet = sb("bet", [128, 1])
        q_s = sb("q_s", [R, HEADS, D])
        k_s = sb("k_s", [R, HEADS, 2, D])
        qk1 = sb("qk1", [128, HEADS * D], F32R)
        qk2 = sb("qk2", [128, HEADS * D], F32R)
        vo = sb("vo", [128, 4, D])
        gq = sb("gq", [128, 2, 4, GCOL])
        xd = sb("xd", [128, 2, GCOL])
        sc = sb("sc", [128, 2, 512])
        ex = sb("ex", [128, 2, 512])
        pn = sb("pn", [128, 2, 512])
        pT = sb("pT", [128, 2, 512])
        vv = sb("vv", [128, 2, 2, 4, D])
        mx = sb("mx", [128, 2, HEADS])
        sm = sb("sm", [128, 2, HEADS])
        rs = sb("rs", [128, 2, HEADS])
        oT = sb("oT", [128, NPAIR * T])
        w1_s = sb("w1_s", [128, EXPERTS * HID])
        w1a = sb("w1a", [128, EXPERTS * HID], F32R)
        w1b = sb("w1b", [128, EXPERTS * HID], F32R)
        b1_s = sb("b1_s", [HID, EXPERTS])
        b1f = sb("b1f", [HID, EXPERTS])
        w2_s = sb("w2_s", [HID, EXPERTS, D])
        b2_s = sb("b2_s", [24, D])
        b2r = sb("b2r", [24, D])
        b2p = sb("b2p", [24, 3, D], BF16)
        wr_s = sb("wr_s", [128, EXPERTS])
        wra = sb("wra", [128, EXPERTS], F32R)
        wrb = sb("wrb", [128, EXPERTS], F32R)
        br_s = sb("br_s", [128, EXPERTS])
        brf = sb("brf", [128, EXPERTS])
        lg = sb("lg", [128, 16, EXPERTS])
        lg2 = sb("lg2", [128, 16, EXPERTS])
        oh1 = sb("oh1", [128, 16, EXPERTS])
        oh2 = sb("oh2", [128, 16, EXPERTS])
        ca = sb("ca", [128, 16, EXPERTS])
        top1 = sb("top1", [128, 16])
        top2 = sb("top2", [128, 16])
        at = sb("at", [128, 16])
        lead = sb("lead", [128, 2, 16])
        g1 = sb("g1", [128, 16])
        g2 = sb("g2", [128, 16])
        gp = sb("gp", [128, 16, 3, EXPERTS], BF16)
        gT = sb("gT", [24, TOK], BF16)
        gTs = sb("gTs", [24, 2 * QCOL], BF16)
        banks = ctx.enter_context(nc.psum_tensor("banks", [128, 8, 512], F32))
        ps = [banks[:, b, :] for b in range(8)]
        VPB, TB, OB, SIDE = ps[4], ps[5], ps[6], ps[7]
        YB = ps[6]

        ld_x = [sem(f"ld_x{c}") for c in range(4)]
        ld_row, ld_con, ld_tok, ld_att, ld_ffn, ld_ffp = (sem(n) for n in ("ld_row", "ld_con", "ld_tok", "ld_att", "ld_ffn", "ld_ffp"))
        zeroed, consts, wtok_sb, wprep, bias_mm, bias_sb = (sem(n) for n in ("zeroed", "consts", "wtok_sb", "wprep", "bias_mm", "bias_sb"))
        t0_mm, t0_act, t0_dve, t1_mm, t1_act, t1_dve = (sem(n) for n in ("t0_mm", "t0_act", "t0_dve", "t1_mm", "t1_act", "t1_dve"))
        ft_mm, ft_sb, mean_mm, h_mm, h_sb = (sem(n) for n in ("ft_mm", "ft_sb", "mean_mm", "h_mm", "h_sb"))
        qk_mm, qk_half, qk_sb = sem("qk_mm"), sem("qk_half"), sem("qk_sb")
        dve_step = sem("dve_step")
        centred, squared, normed, part1, part2 = (sem(n) for n in ("centred", "squared", "normed", "part1", "part2"))
        xt_mm, xt_act, xt_dve = sem("xt_mm"), sem("xt_act"), sem("xt_dve")
        x_mm, x_sb, prep_mm, prep_sb = sem("x_mm"), sem("x_sb"), sem("prep_mm"), sem("prep_sb")
        s_mm, mx_done, s_sub, e_done, sm_done, r_done, p_norm = (sem(n) for n in (
            "s_mm", "mx_done", "s_sub", "e_done", "sm_done", "r_done", "p_norm"))
        t_mm, t_sb, v_mm, v_sb, o_mm, o_sb = (sem(n) for n in ("t_mm", "t_sb", "v_mm", "v_sb", "o_mm", "o_sb"))
        side_mm, side_free = sem("side_mm"), sem("side_free")
        lead_v, lead_t, gate_sp = sem("lead_v"), sem("lead_t"), sem("gate_sp")
        gts_sb, u_mm, g_mm, hid_sb, hw_sb, y_mm, y_sb, yt_mm, h_out, stored = (sem(n) for n in (
            "gts_sb", "u_mm", "g_mm", "hid_sb", "hw_sb", "y_mm", "y_sb", "yt_mm", "h_out", "stored"))
        block = ctx.enter_context(nc.Block())

        def halfs(t, f):
            return t[:, 2 * f:2 * f + 2].rearrange("p k a j e -> p (k a j) e")

        def attention(slot, side):
            with slot.engine.Fori(0, NG // 4) as i:
                for q in range(2):
                    for p in range(GP):
                        slot(i * 2 + q, q, p, i * (2 * GP) + (q * GP + p), 2)
            for g in range(NG // 2, NG):
                for p in range(GP):
                    slot(g, g % 2, p, g * GP + p, min(2, NG - 1 - g))
                    side(0, (g - NG // 2) * GP + p)

        def feed_forward(step, side):
            for k in range(NQ // 2):
                step(k, lambda n: side(1, 8 * k + n))
            with step.engine.Fori(NQ // 2, NQ) as k:
                step(k, lambda n: None)

        def on(engine):
            def mark(f):
                f.engine = engine
                return f
            return mark

        @block.sync
        def _(sp):
            xv = x.rearrange("b c r w -> r (b c) w")
            for c in range(4):
                for f in range(HALVES):
                    b = 32 * f + 8 * c
                    sp.dma_start(img[:, b:b + 8, :], xv[:, b:b + 8, :]).then_inc(ld_x[c], 16)
            sp.dma_start(w1_s[0:D, :].rearrange("d (n k) -> d n k", k=HID), w1.rearrange("n d k -> d n k")).then_inc(ld_ffn, 16)
            sp.dma_start(w1_s[D:128, :].rearrange("d (n k) -> d n k", k=HID), w1.rearrange("n d k -> d n k")).then_inc(ld_ffn, 16)
            sp.dma_start(w2_s[:, :, :], w2.rearrange("n k d -> k n d")).then_inc(ld_ffn, 16)
            sp.dma_start(pick_f[:, :, :], pick_c).then_inc(ld_ffn, 16)
            ov = out.rearrange("(f m a) (i q j) e -> f q a m i (j e)", f=HALVES, a=2, i=GRID, q=2)
            for k in range(NQ):
                sp.wait_ge(h_out, k + 1)
                for a in range(2):
                    sp.dma_start(ov[k // 2, k % 2, a], h[:, k, a, :, :].rearrange("p j e -> p (j e)")).then_inc(stored, 16)
            sp.wait_ge(stored, 32 * NQ)

        @block.gpsimd
        def _(pool):
            pool.memset(wrep[:, :], 0.0).then_inc(zeroed, 1)
            pool.wait_ge(zeroed, 1)
            for f in range(HALVES):
                pool.dma_start(wrep[64 * f:64 * f + MAPS * GRID, :], tok_w.unsqueeze(1).to_broadcast([MAPS, GRID, D])).then_inc(ld_tok, 16)
                pool.dma_start(wrep[64 * f + MAPS * GRID:64 * f + MAPS * GRID + 1, :], tok_b.rearrange("(a e) -> a e", a=1)).then_inc(ld_tok, 16)
            for f in range(2):
                c = slice(64 * f, 64 * f + 64)
                pool.dma_start(gam[c, :], gamma.rearrange("(e a) -> e a", a=1)).then_inc(ld_ffp, 16)
                pool.dma_start(bet[c, :], beta.rearrange("(e a) -> e a", a=1)).then_inc(ld_ffp, 16)
                pool.dma_start(wr_s[c, :], wr).then_inc(ld_ffp, 16)
            pool.dma_start(br_s[:, :], br.rearrange("(a e) -> a e", a=1).to_broadcast([128, EXPERTS])).then_inc(ld_ffp, 16)
            for c in range(3):
                pool.dma_start(b2_s[8 * c:8 * c + 8, :], b2).then_inc(ld_ffp, 16)
            with nc.allow_non_contiguous_dma(reason="4 KB of biases, hidden unit on partitions"):
                pool.dma_start(b1_s[:, :], b1.rearrange("n k -> k n")).then_inc(ld_ffp, 16)

            def norm(n, b):
                pool.wait_ge(r_done, n + 1)
                pool.tensor_tensor(
                    pn[:, b, :].rearrange("p (q o u) -> p o q u", o=2, u=T),
                    ex[:, b, :].rearrange("p (o q u) -> p o q u", o=2, u=T),
                    rs[:, b, :].rearrange("p (o q) -> p o q", o=2).unsqueeze(3).to_broadcast([128, 2, 4, T]),
                    ALU.mult).then_inc(p_norm, 1)

            norm(0, 0)

            @on(pool)
            def slot(g, gb, p, n, left):
                if p < GP - 1 or left >= 1:
                    norm(n + 1, (p + 1) % 2)

            attention(slot, lambda f, step: None)

        @block.scalar
        def _(act):
            act.dma_start(rowop[:, :], row_ops).then_inc(ld_row, 16)
            act.dma_start(ident[:, :], ident_c).then_inc(ld_con, 16)
            act.dma_start(colop[:, :, :], col_ops).then_inc(ld_con, 16)
            act.dma_start(mask[:, :], mask_c).then_inc(ld_con, 16)
            act.dma_start(one[:, :], one_c).then_inc(ld_con, 16)
            act.dma_start(fold_f[:, :], fold_c).then_inc(ld_con, 16)
            act.dma_start(rev[:, :], rev_c).then_inc(ld_con, 16)
            act.dma_start(q_s[:, :, :], wq.rearrange("h r d -> r h d")).then_inc(ld_att, 16)
            for c in range(2):
                act.dma_start(k_s[:, :, c, :], wk.rearrange("h r d -> r h d")).then_inc(ld_att, 16)
            for o in range(2):
                act.dma_start(vo[64 * o:64 * o + 64, :, :], wvo.rearrange("(q o) d e -> o d q e", o=2)[o]).then_inc(ld_att, 16)
            for c in (1, 3):
                act.wait_ge(t0_mm, c + 1)
                act.activation(t0[:, 4 * c:4 * c + 4, :].rearrange("p m w -> p (m w)"), ps[c][:, 0:4 * PX], ACT.Copy).then_inc(t0_act, 1)
            for c in (1, 3):
                act.wait_ge(t1_mm, c + 1)
                act.activation(t1[:, :, 4 * c:4 * c + 4, :].rearrange("w r m i -> w m r i"),
                               ps[4 + c][0:PX, :].rearrange("w (m r i) -> w m r i", m=4, i=GRID), ACT.Copy).then_inc(t1_act, 1)
            act.wait_ge(qk_mm, 1)
            act.activation(qk1[:, :], ps[1][:, :], ACT.Copy, scale=1.0 / 8.0).then_inc(qk_half, 1)

            def residual(f):
                for a in range(2):
                    act.wait_ge(h_mm, 2 * f + a + 1)
                    act.wait_ge(centred, 2 * f + a + 1)
                    act.activation(h[:, 2 * f:2 * f + 2, a, :, :], ps[2 + 2 * f + a][:, :].rearrange("p (q j e) -> p q j e", q=2, e=D),
                                   ACT.Copy).then_inc(h_sb, 1)

            def squares(f, count):
                act.wait_ge(centred, count)
                act.activation(halfs(sq, f), halfs(xc, f), ACT.Square).then_inc(squared, 1)

            def first_part(f, count):
                act.wait_ge(normed, count)
                act.activation(x12[:, 16 * f:16 * f + 16, 0, :].bitcast(F32R), halfs(sq, f), ACT.Copy).then_inc(part1, 1)

            squares(0, 2)
            squares(1, 4)
            first_part(0, 1)
            residual(0)
            residual(1)
            first_part(1, 2)
            for c in (1, 3, 5, 7):
                act.wait_ge(xt_mm, c + 1)
                f, q, a = c // 4, (c // 2) % 2, c % 2
                act.activation(
                    xT[:, :].rearrange("p (f m a j i) -> p f a j m i", f=2, m=PAIRS, a=2, i=GRID)[:, f, a, 4 * q:4 * q + 4],
                    ps[c % 4][:, :].rearrange("p (j m i) -> p j m i", j=4, i=GRID), ACT.Copy).then_inc(xt_act, 1)

            def x_twice(g, gb):
                act.wait_ge(x_mm, g + 1)
                act.activation(xd[:, gb, :], SIDE[:, :], ACT.Copy).then_inc(x_sb, 1)

            def prep(k, gb, q):
                act.wait_ge(prep_mm, k + 1)
                act.activation(gq[:, gb, q, :], VPB[:, :], ACT.Copy).then_inc(prep_sb, 1)

            def exps(n, b):
                act.wait_ge(s_sub, n + 1)
                act.activation(ex[:, b, :], sc[:, b, :], ACT.Exp).then_inc(e_done, 1)

            def values(n, b):
                act.wait_ge(v_mm, n + 1)
                act.activation(vv[:, b].rearrange("p a q e -> p (a q e)"), VPB[:, :], ACT.Copy).then_inc(v_sb, 1)

            x_twice(0, 0)
            for k in range(6):
                prep(k, k // 4, k % 4)
            exps(0, 0)
            values(0, 0)
            exps(1, 1)

            @on(act)
            def slot(g, gb, p, n, left):
                act.wait_ge(t_mm, n + 1)
                act.activation(pT[:, p % 2, :], TB[:, :], ACT.Copy).then_inc(t_sb, 1)
                if p == 0 and left >= 1:
                    x_twice(g + 1, 1 - gb)
                if p < GP - 1 or left >= 1:
                    values(n + 1, (p + 1) % 2)
                if p < 2 and left >= 1:
                    prep(n + 6, 1 - gb, p + 2)
                if p >= 2 and left >= 2:
                    prep(n + 6, gb, p - 2)
                if p < 2 or left >= 1:
                    exps(n + 2, p % 2)
                if p == GP - 1:
                    act.wait_ge(o_mm, g + 1)
                    act.activation(
                        oT[:, :].rearrange("p (j c) -> p j c", j=GRID)[:, :, bass.ds(g * (GP * GRID), GP * GRID)].rearrange("p j (m i) -> p j m i", i=GRID),
                        OB[:, 0:GP * T].rearrange("p (m j i) -> p j m i", m=GP, j=GRID), ACT.Copy).then_inc(o_sb, 1)

            def side(f, step):
                used = SIDE_USES * f
                if step == 3:
                    squares(f, 5 + f)
                if step == 7:
                    first_part(f, 3 + f)
                if 9 <= step < 13:
                    c = step - 9
                    act.wait_ge(side_mm, used + 3 + c)
                    act.activation(xfT[:, f * 2048 + c * 512:f * 2048 + c * 512 + 512], SIDE[:, :], ACT.Copy).then_inc(side_free, 1)
                if step == 14:
                    act.wait_ge(lead_v, f + 1)
                    act.activation(lead[:, 1, :], lead[:, 0, :], ACT.Tanh, scale=0.5).then_inc(lead_t, 1)
                if step == 15:
                    for c in range(2):
                        act.wait_ge(side_mm, used + 8 + c)
                        act.activation(gT[:, f * 2048 + c * 1024:f * 2048 + c * 1024 + 1024], SIDE[0:24, :].bitcast(BF16), ACT.Copy).then_inc(side_free, 1)

            attention(slot, side)

            @on(act)
            def step(k, side):
                for n in range(EXPERTS):
                    for a in range(2):
                        b = 2 * (n % 2) + a
                        act.wait_ge(u_mm, k * 16 + (2 * n + a + 1))
                        act.activation(hid[:, b, :], ps[b][:, :], ACT.Gelu, bias=b1f[:, n:n + 1]).then_inc(hid_sb, 1)
                    side(n)
                act.wait_ge(y_mm, k * 8 + 8)
                act.activation(yT[:, :], YB[:, :], ACT.Copy).then_inc(y_sb, 1)

            feed_forward(step, side)

        @block.vector
        def _(dve):
            steps = [0]

            def link(ins):
                steps[0] += 1
                ins.then_inc(dve_step, 1)
                dve.wait_ge(dve_step, steps[0])

            def rsqrt(y, v, half_v, t):
                link(dve.tensor_scalar(half_v, v, -0.5, None, ALU.mult))
                link(dve.tensor_scalar(y.bitcast(I32), v.bitcast(I32), 1, None, ALU.logical_shift_right))
                link(dve.tensor_scalar(y.bitcast(I32), y.bitcast(I32), -1.0, float(MAGIC), ALU.mult, ALU.add))
                for _ in range(3):
                    link(dve.tensor_tensor(t, y, y, ALU.mult))
                    link(dve.tensor_tensor(t, t, half_v, ALU.mult))
                    link(dve.scalar_tensor_tensor(y, t, 1.5, y, op0=ALU.add, op1=ALU.mult))

            dve.wait_ge(ld_con, 16 * 6)
            dve.tensor_copy(identb[:, :], ident[:, :]).then_inc(consts, 1)
            dve.tensor_copy(fold[:, :], fold_f[:, :]).then_inc(consts, 1)
            dve.wait_ge(ld_tok, 64)
            link(dve.reduce_sum(wavg[:, :], wrep[:, :], axis=AX.X))
            link(dve.tensor_scalar(wavg[:, :], wavg[:, :], 1.0 / D, None, ALU.mult))
            dve.tensor_scalar(wmean[:, :], mask[:, :], wavg[:, :], None, ALU.mult).then_inc(wtok_sb, 1)
            dve.tensor_tensor(wtok[:, :, :], wrep[:, :].unsqueeze(1).to_broadcast([128, GRID, D]),
                              mask[:, :].unsqueeze(2).to_broadcast([128, GRID, D]), ALU.mult).then_inc(wtok_sb, 1)
            for c in (0, 2):
                dve.wait_ge(t0_mm, c + 1)
                dve.tensor_copy(t0[:, 4 * c:4 * c + 4, :].rearrange("p m w -> p (m w)"), ps[c][:, 0:4 * PX]).then_inc(t0_dve, 1)
            for c in (0, 2):
                dve.wait_ge(t1_mm, c + 1)
                dve.tensor_copy(t1[:, :, 4 * c:4 * c + 4, :].rearrange("w r m i -> w m r i"),
                                ps[4 + c][0:PX, :].rearrange("w (m r i) -> w m r i", m=4, i=GRID)).then_inc(t1_dve, 1)
            dve.wait_ge(ft_mm, 1)
            dve.tensor_scalar(feat[:, :], ps[0][:, 0:256], one[:, :], None, ALU.add).then_inc(ft_sb, 1)
            dve.wait_ge(qk_half, 1)
            dve.scalar_tensor_tensor(qk2[:, :], ps[1][:, :], 1.0 / 8.0, qk1[:, :].bitcast(F32),
                                     op0=ALU.mult, op1=ALU.subtract).then_inc(qk_sb, 1)

            dve.wait_ge(mean_mm, 1)
            link(dve.tensor_copy(mean[:, :].rearrange("p (f q a j) -> p f q a j", f=2, q=2, a=2)[:, 0],
                                 ps[0][:, 0:16].rearrange("p (a q j) -> p q a j", a=2, q=2)))
            link(dve.tensor_copy(mean[:, :].rearrange("p (f q a j) -> p f q a j", f=2, q=2, a=2)[:, 1],
                                 ps[6][:, 0:16].rearrange("p (a q j) -> p q a j", a=2, q=2)))
            for f in range(HALVES):
                for a in range(2):
                    dve.wait_ge(h_mm, 2 * f + a + 1)
                    for q in range(2):
                        k = 2 * f + q
                        ins = dve.tensor_tensor(
                            xc[:, k, a, :, :], ps[2 + 2 * f + a][:, 256 * q:256 * q + 256].rearrange("p (j e) -> p j e", j=4),
                            mean[:, 8 * k + 4 * a:8 * k + 4 * a + 4].unsqueeze(2).to_broadcast([128, 4, D]), ALU.subtract)
                    ins.then_inc(centred, 1)

            def scale(f, count, one_eps, eps):
                c = slice(16 * f, 16 * f + 16)
                dve.wait_ge(squared, count)
                link(dve.reduce_sum(var[:, c], halfs(sq, f), axis=AX.X))
                link(dve.tensor_scalar(var[:, c], var[:, c], one_eps / D, eps, ALU.mult, ALU.add))

            def newton(f):
                c = slice(16 * f, 16 * f + 16)
                rsqrt(rstd[:, c], var[:, c], hvar[:, c], tmp[:, c])

            def apply(f):
                c = slice(16 * f, 16 * f + 16)
                dve.tensor_tensor(halfs(sq, f), halfs(xc, f), rstd[:, c].unsqueeze(2).to_broadcast([128, 16, D]),
                                  ALU.mult).then_inc(normed, 1)

            def second_part(f, count):
                c = slice(16 * f, 16 * f + 16)
                dve.wait_ge(part1, count)
                dve.tensor_tensor(x12[:, c, 1, :], halfs(sq, f), x12[:, c, 0, :], ALU.subtract).then_inc(part2, 1)

            scale(0, 1, 1.0, EPS)
            newton(0)
            apply(0)
            scale(1, 2, 1.0, EPS)
            second_part(0, 1)
            newton(1)
            apply(1)
            for c in (0, 2):
                dve.wait_ge(xt_mm, c + 1)
                f, q, a = c // 4, (c // 2) % 2, c % 2
                dve.tensor_copy(
                    xT[:, :].rearrange("p (f m a j i) -> p f a j m i", f=2, m=PAIRS, a=2, i=GRID)[:, f, a, 4 * q:4 * q + 4],
                    ps[c % 4][:, :].rearrange("p (j m i) -> p j m i", j=4, i=GRID)).then_inc(xt_dve, 1)
            second_part(1, 2)
            for c in (4, 6):
                dve.wait_ge(xt_mm, c + 1)
                f, q, a = c // 4, (c // 2) % 2, c % 2
                dve.tensor_copy(
                    xT[:, :].rearrange("p (f m a j i) -> p f a j m i", f=2, m=PAIRS, a=2, i=GRID)[:, f, a, 4 * q:4 * q + 4],
                    ps[c % 4][:, :].rearrange("p (j m i) -> p j m i", j=4, i=GRID)).then_inc(xt_dve, 1)

            def less_max(n, b):
                dve.wait_ge(s_mm, n + 1)
                raw = banks[:, 2 * b:2 * b + 2, 0:256].rearrange("p o (q u) -> p o q u", u=T)
                peak = mx[:, b, :].rearrange("p (o q) -> p o q", o=2)
                dve.reduce_max(peak, raw, axis=AX.X).then_inc(mx_done, 1)
                dve.wait_ge(mx_done, n + 1)
                dve.tensor_tensor(sc[:, b, :].rearrange("p (o q u) -> p o q u", o=2, u=T), raw,
                                  peak.unsqueeze(3).to_broadcast([128, 2, 4, T]), ALU.subtract).then_inc(s_sub, 1)

            def sums(n, b):
                dve.wait_ge(e_done, n + 1)
                dve.reduce_sum(sm[:, b, :], ex[:, b, :].rearrange("p (h u) -> p h u", u=T), axis=AX.X).then_inc(sm_done, 1)
                dve.wait_ge(sm_done, n + 1)
                dve.reciprocal(rs[:, b, :], sm[:, b, :]).then_inc(r_done, 1)

            less_max(0, 0)
            sums(0, 0)
            less_max(1, 1)

            @on(dve)
            def slot(g, gb, p, n, left):
                if p < GP - 1 or left >= 1:
                    sums(n + 1, (p + 1) % 2)
                if p < 2 or left >= 1:
                    less_max(n + 2, p % 2)

            def weights(step):
                if step == 0:
                    dve.wait_ge(ld_ffn, 16 * 4)
                    dve.wait_ge(ld_ffp, 16 * 11)
                    link(dve.tensor_scalar(w1a[:, :], w1_s[:, :], gam[:, :], None, ALU.mult))
                    dve.scalar_tensor_tensor(w1b[:, :], w1_s[:, :], gam[:, :], w1a[:, :].bitcast(F32),
                                             op0=ALU.mult, op1=ALU.subtract).then_inc(wprep, 1)
                if step == 1:
                    link(dve.tensor_scalar(wra[:, :], wr_s[:, :], gam[:, :], None, ALU.mult))
                    dve.scalar_tensor_tensor(wrb[:, :], wr_s[:, :], gam[:, :], wra[:, :].bitcast(F32),
                                             op0=ALU.mult, op1=ALU.subtract).then_inc(wprep, 1)
                    dve.tensor_copy(pick[:, :, :], pick_f[:, :, :]).then_inc(wprep, 1)
                    link(dve.tensor_copy(b2p[:, 0, :], b2_s[:, :]))
                    link(dve.tensor_tensor(b2r[:, :], b2_s[:, :], b2p[:, 0, :], ALU.subtract))
                    link(dve.tensor_copy(b2p[:, 1, :], b2r[:, :]))
                    dve.tensor_tensor(b2p[:, 2, :], b2r[:, :], b2p[:, 1, :], ALU.subtract).then_inc(wprep, 1)

            def gates(f, part):
                E3 = [128, 16, EXPERTS]
                up = lambda ap: ap.unsqueeze(2).to_broadcast(E3)
                across = lambda ap: ap.unsqueeze(1).to_broadcast(E3)

                def first_largest(src, onehot, top):
                    link(dve.reduce_max(top[:, :], src[:, :, :], axis=AX.X))
                    link(dve.tensor_tensor(onehot[:, :, :], src[:, :, :], up(top[:, :]), ALU.is_equal))
                    link(dve.tensor_tensor(ca[:, :, :], onehot[:, :, :], across(rev[:, :]), ALU.mult))
                    link(dve.reduce_max(at[:, :], ca[:, :, :], axis=AX.X))
                    link(dve.tensor_tensor(onehot[:, :, :], ca[:, :, :], up(at[:, :]), ALU.is_equal))

                if part == 0:
                    dve.wait_ge(side_mm, SIDE_USES * f + 7)
                    ins = dve.tensor_tensor(lg[:, :, :], SIDE[:, 0:128].rearrange("p (s n) -> p s n", n=EXPERTS),
                                            across(brf[:, :]), ALU.add)
                    ins.then_inc(side_free, 1)
                    dve.wait_ge(side_free, SIDE_USES * f + 7)
                    first_largest(lg, oh1, top1)
                if part == 1:
                    link(dve.scalar_tensor_tensor(lg2[:, :, :], oh1[:, :, :], BIG, lg[:, :, :], op0=ALU.mult, op1=ALU.add))
                    first_largest(lg2, oh2, top2)
                    dve.tensor_tensor(lead[:, 0, :], top1[:, :], top2[:, :], ALU.subtract).then_inc(lead_v, 1)
                if part == 2:
                    dve.wait_ge(lead_t, f + 1)
                    link(dve.tensor_scalar(g1[:, :], lead[:, 1, :], 0.5, 0.5, ALU.mult, ALU.add))
                    link(dve.tensor_scalar(g2[:, :], lead[:, 1, :], -0.5, 0.5, ALU.mult, ALU.add))
                    link(dve.tensor_tensor(lg[:, :, :], oh1[:, :, :], up(g1[:, :]), ALU.mult))
                    link(dve.tensor_tensor(lg2[:, :, :], oh2[:, :, :], up(g2[:, :]), ALU.mult))
                    link(dve.tensor_tensor(ca[:, :, :], lg[:, :, :], lg2[:, :, :], ALU.add))
                    link(dve.tensor_copy(gp[:, :, 0, :], ca[:, :, :]))
                    link(dve.tensor_tensor(lg[:, :, :], ca[:, :, :], gp[:, :, 0, :], ALU.subtract))
                    link(dve.tensor_copy(gp[:, :, 1, :], lg[:, :, :]))
                    dve.tensor_tensor(gp[:, :, 2, :], lg[:, :, :], gp[:, :, 1, :], ALU.subtract).then_inc(gate_sp, 1)

            def side(f, step):
                c = slice(16 * f, 16 * f + 16)
                used = SIDE_USES * f
                if step < 2:
                    k = 2 * f + step
                    dve.wait_ge(side_mm, used + step + 1)
                    hk = h[:, k].rearrange("p a j e -> p j a e")
                    dve.tensor_tensor(hk, hk, SIDE[:, :].rearrange("p (j a e) -> p j a e", j=4, e=D), ALU.add).then_inc(side_free, 1)
                if step == 2:
                    dve.wait_ge(side_free, used + 2)
                    link(dve.reduce_sum(mean[:, c], halfs(h, f), axis=AX.X))
                    dve.scalar_tensor_tensor(halfs(xc, f), mean[:, c].unsqueeze(2).to_broadcast([128, 16, D]), -1.0 / D,
                                             halfs(h, f), op0=ALU.mult, op1=ALU.add).then_inc(centred, 1)
                if step == 4:
                    scale(f, 3 + f, 1.0 + EPS, EPS * EPS)
                if step == 5:
                    newton(f)
                if step == 6:
                    apply(f)
                if step == 8:
                    second_part(f, 3 + f)
                if f == 0 and step in (10, 11):
                    weights(step - 10)
                if f == 0 and step == 12:
                    dve.wait_ge(bias_mm, 1)
                    dve.tensor_tensor(b1f[:, :], b1_s[:, :], ps[7][:, 128:136], ALU.add).then_inc(bias_sb, 1)
                    dve.tensor_tensor(brf[:, :], br_s[:, :], ps[7][:, 136:144], ALU.add).then_inc(bias_sb, 1)
                if step >= 13:
                    gates(f, step - 13)

            attention(slot, side)

            @on(dve)
            def step(k, side):
                if not isinstance(k, int):
                    dve.wait_ge(y_mm, k * 8)
                elif k:
                    dve.wait_ge(y_mm, k * 8)
                else:
                    dve.wait_ge(side_free, SIDE_USES)
                dve.tensor_copy(gTs[:, :], gT[:, bass.ds(k * (2 * QCOL), 2 * QCOL)]).then_inc(gts_sb, 1)

                def join(k):
                    dve.wait_ge(yt_mm, k + 1)
                    hk = h[:, :, :, :, :].rearrange("p k a j e -> p (k a j e)")[:, bass.ds(k * 512, 512)].rearrange(
                        "p (a j e) -> p j a e", a=2, e=D)
                    dve.tensor_tensor(hk, hk, ps[7][:, :].rearrange("p (j a e) -> p j a e", j=4, e=D), ALU.add).then_inc(h_out, 1)

                for n in range(EXPERTS):
                    for a in range(2):
                        b = 2 * (n % 2) + a
                        dve.wait_ge(hid_sb, k * 16 + (2 * n + a + 1))
                        dve.wait_ge(g_mm, k * 16 + (2 * n + a + 1))
                        if n >= 2:
                            dve.wait_ge(y_mm, k * 8 + (n - 1))
                        dve.tensor_tensor(hw[:, b, :], hid[:, b, :], ps[4 + a][:, :], ALU.mult).then_inc(hw_sb, 1)
                    side(n)
                join(k)

            feed_forward(step, side)

        @block.tensor
        def _(pe):
            pe.wait_ge(ld_row, 16)
            for c in range(4):
                pe.wait_ge(ld_x[c], 32)
                for q in range(4):
                    b = 32 * (q // 2) + 8 * c + q % 2
                    last = pe.matmul(banks[32 * q:32 * q + 32, c, 0:4 * PX], rowop[:, :], img[:, b:b + 7:2, :], start=True, stop=True)
                last.then_inc(t0_mm, 1)
            pe.wait_ge(ld_con, 16 * 6)
            for c in range(4):
                pe.wait_ge((t0_dve, t0_act)[c % 2], c // 2 + 1)
                for m in range(4):
                    last = pe.transpose(ps[4 + c][0:PX, 128 * m:128 * m + 128], t0[:, 4 * c + m, :], ident[:, :])
                last.then_inc(t1_mm, 1)
            pe.wait_ge(ld_att, 80)
            for hd in range(HEADS):
                last = pe.matmul(ps[1][:, hd * D:(hd + 1) * D], k_s[:, hd, :, :], q_s[:, hd, :], start=True, stop=True)
            last.then_inc(qk_mm, 1)
            pe.wait_ge(t1_act, 2)
            pe.wait_ge(t1_dve, 2)
            tv = t1[:, :, :, :].rearrange("w (f a r) m i -> w f a r (m i)", f=2, a=2)
            for r in range(4):
                for f in range(HALVES):
                    last = pe.matmul(ps[0][64 * f:64 * f + 64, 0:256], colop[:, r, :], tv[:, f, :, r, :], start=r == 0, stop=r == 3)
            last.then_inc(ft_mm, 1)
            pe.wait_ge(ft_sb, 1)
            pe.wait_ge(wtok_sb, 2)
            for m in range(4):
                f, a = m // 2, m % 2
                last = pe.matmul(ps[6 * f][:, 8 * a:8 * a + 8], feat[64 * f:64 * f + 64, 128 * a:128 * a + 128],
                                 wmean[64 * f:64 * f + 64, :], start=True, stop=True)
            last.then_inc(mean_mm, 1)
            for m in range(4):
                f, a = m // 2, m % 2
                pe.matmul(ps[2 + m][:, :], feat[64 * f:64 * f + 64, 128 * a:128 * a + 128],
                          wtok[64 * f:64 * f + 64, :, :].rearrange("k j e -> k (j e)"), start=True, stop=True).then_inc(h_mm, 1)
            pe.wait_ge(h_sb, 4)
            for c in range(8):
                if c % 4 == 0:
                    pe.wait_ge(part2, c // 4 + 1)
                if c >= 4:
                    pe.wait_ge((xt_dve, xt_act)[c % 2], (c - 4) // 2 + 1)
                for j in range(4):
                    last = pe.transpose(ps[c % 4][:, 128 * j:128 * j + 128], x12[:, 4 * c + j, :, :].rearrange("p a e -> p (a e)"), ident[:, :])
                last.then_inc(xt_mm, 1)
            pe.wait_ge(consts, 2)
            pe.wait_ge(qk_sb, 1)
            pe.wait_ge(xt_act, 4)
            pe.wait_ge(xt_dve, 4)

            def x_twice(g):
                pe.matmul(SIDE[:, :], fold[:, :], xT[:, bass.ds(g * GCOL, GCOL)], start=True, stop=True).then_inc(x_mm, 1)

            def prep(g, q):
                cols = xT[:, bass.ds(g * GCOL, GCOL)]
                w = slice(128 * q, 128 * q + 128)
                pe.matmul(VPB[:, :], qk1[:, w], cols, start=True, stop=False)
                pe.matmul(VPB[:, :], qk2[:, w], cols, start=False, stop=True).then_inc(prep_mm, 1)

            def scores(n, gb, p, b):
                for o, a in ((0, 0), (1, 1), (1, 0), (0, 1)):
                    t0 = 128 * p + 64 * a
                    last = pe.matmul(banks[64 * a:64 * a + 64, 2 * b + o, 0:256], xd[64 * o:64 * o + 64, gb, t0:t0 + 64],
                                     gq[64 * o:64 * o + 64, gb, :, t0:t0 + 64], start=True, stop=True)
                last.then_inc(s_mm, 1)

            def values(n, gb, p):
                for a in range(2):
                    for o in range(2):
                        t0 = 128 * p + 64 * a
                        last = pe.matmul(VPB[64 * o:64 * o + 64, 256 * a:256 * a + 256], xd[64 * o:64 * o + 64, gb, t0:t0 + 64],
                                         vo[64 * o:64 * o + 64, :, :].rearrange("p q e -> p (q e)"), start=True, stop=True)
                last.then_inc(v_mm, 1)

            x_twice(0)
            for k in range(6):
                if k:
                    pe.wait_ge(prep_sb, k)
                prep(k // 4, k % 4)
                if k == 4:
                    pe.wait_ge(x_sb, 1)
                    scores(0, 0, 0, 0)
            scores(1, 0, 1, 1)
            pe.wait_ge(prep_sb, 6)
            values(0, 0, 0)

            @on(pe)
            def slot(g, gb, p, n, left):
                total = NPAIR
                if isinstance(n, int):
                    pe.wait_ge(prep_sb, min(n + 6, total))
                else:
                    pe.wait_ge(prep_sb, n + 6)
                if p == 2 and left >= 1:
                    pe.wait_ge(x_sb, g + 2)
                pe.wait_ge(v_sb, n + 1)
                pe.wait_ge(p_norm, n + 1)
                for q in range(4):
                    last = pe.transpose(TB[:, 128 * q:128 * q + 128], pn[:, p % 2, 128 * q:128 * q + 128], ident[:, :])
                last.then_inc(t_mm, 1)
                if p == 0 and left >= 1:
                    if isinstance(n, int):
                        pe.wait_ge(side_free, side_used(n))
                    x_twice(g + 1)
                if p < GP - 1:
                    values(n + 1, gb, p + 1)
                elif left >= 1:
                    values(n + 1, 1 - gb, 0)
                if p < 2:
                    scores(n + 2, gb, p + 2, p % 2)
                elif left >= 1:
                    scores(n + 2, 1 - gb, p - 2, p % 2)
                if (p < 2 and left >= 1) or left >= 2:
                    pe.wait_ge(v_sb, n + 2)
                    prep(g + 1 if p < 2 else g + 2, (p + 2) % 4)
                pe.wait_ge(t_sb, n + 1)
                for q in range(4):
                    for a in range(2):
                        last = pe.matmul(OB[64 * a:64 * a + 64, T * p:T * p + T], vv[:, p % 2, a, q, :],
                                         pT[:, p % 2, 128 * q + 64 * a:128 * q + 64 * a + 64], start=q == 0, stop=q == 3)
                if p == GP - 1:
                    last.then_inc(o_mm, 1)

            def side_used(n):
                return sum(1 for s in range(n - NPAIR // 2) if s < 2 or 9 <= s < 14)

            def side(f, step):
                used = SIDE_USES * f
                if step < 2:
                    if step == 0:
                        pe.wait_ge(o_sb, 4 * f + 4)
                        if f == 0:
                            pe.wait_ge(x_sb, NG // 2 + 2)
                    if used + step:
                        pe.wait_ge(side_free, used + step)
                    for j in range(4):
                        c = 256 * (4 * step + j) + 128 * f
                        last = pe.transpose(SIDE[:, 128 * j:128 * j + 128], oT[:, c:c + 128], ident[:, :])
                    last.then_inc(side_mm, 1)
                if 9 <= step < 13:
                    c = step - 9
                    if c == 0:
                        pe.wait_ge(part2, 3 + f)
                    if f == 0 and step == 12:
                        pe.wait_ge(x_sb, NG)
                    pe.wait_ge(side_free, used + 2 + c)
                    for j in range(4):
                        last = pe.transpose(SIDE[:, 128 * j:128 * j + 128],
                                            x12[:, 16 * f + 4 * c + j, :, :].rearrange("p a e -> p (a e)"), ident[:, :])
                    last.then_inc(side_mm, 1)
                if step == 13:
                    if f == 0:
                        pe.wait_ge(wprep, 4)
                        pe.wait_ge(side_free, used + 6)
                        for n in range(EXPERTS):
                            pe.matmul(SIDE[:, 128 + n:129 + n], w1_s[0:D, n * HID:(n + 1) * HID], bet[0:D, :], start=True, stop=True)
                        pe.matmul(SIDE[:, 136:144], bet[0:D, :].to_broadcast([D, 128]), wr_s[0:D, :], start=True, stop=True).then_inc(bias_mm, 1)
                        pe.wait_ge(bias_sb, 2)
                    pe.wait_ge(side_free, used + 6)
                    for s in range(16):
                        t = f * 2048 + 128 * s
                        pe.matmul(SIDE[:, 8 * s:8 * s + 8], xfT[:, t:t + 128], wra[:, :], start=True, stop=False)
                        last = pe.matmul(SIDE[:, 8 * s:8 * s + 8], xfT[:, t:t + 128], wrb[:, :], start=False, stop=True)
                    last.then_inc(side_mm, 1)
                if step == 15:
                    pe.wait_ge(gate_sp, f + 1)
                    for c in range(2):
                        pe.wait_ge(side_free, used + 7 + c)
                        for s in range(8):
                            last = pe.transpose(SIDE[0:24, :].bitcast(BF16)[:, 128 * s:128 * s + 128],
                                                gp[:, 8 * c + s, :, :].rearrange("p c n -> p (c n)"), identb[:, :])
                        last.then_inc(side_mm, 1)

            attention(slot, side)

            @on(pe)
            def step(k, side):
                def hidden(n):
                    for a in range(2):
                        b = 2 * (n % 2) + a
                        if n >= 2:
                            pe.wait_ge(hid_sb, k * 16 + (2 * (n - 2) + a + 1))
                        cols = xfT[:, bass.ds(k * (2 * QCOL) + a * QCOL, QCOL)]
                        pe.matmul(ps[b][:, :], w1a[:, n * HID:(n + 1) * HID], cols, start=True, stop=False)
                        pe.matmul(ps[b][:, :], w1b[:, n * HID:(n + 1) * HID], cols, start=False, stop=True).then_inc(u_mm, 1)

                def spread(n):
                    for a in range(2):
                        if n >= 1:
                            pe.wait_ge(hw_sb, k * 16 + (2 * (n - 1) + a + 1))
                        pe.matmul(ps[4 + a][:, :], pick[:, n, :], gTs[:, a * QCOL:(a + 1) * QCOL], start=True, stop=True).then_inc(g_mm, 1)

                hidden(0)
                pe.wait_ge(gts_sb, k + 1)
                spread(0)
                hidden(1)
                for c in range(3):
                    for a in range(2):
                        pe.matmul(YB[64 * a:64 * a + 64, :], b2p[:, c, :], gTs[:, a * QCOL:(a + 1) * QCOL],
                                  start=c == 0, stop=False)
                for n in range(EXPERTS):
                    if 0 < n < EXPERTS - 1:
                        hidden(n + 1)
                    if n + 1 < EXPERTS:
                        spread(n + 1)
                    pe.wait_ge(hw_sb, k * 16 + (2 * n + 2))
                    for a in range(2):
                        last = pe.matmul(YB[64 * a:64 * a + 64, :], w2_s[:, n, :], hw[:, 2 * (n % 2) + a, :],
                                         start=False, stop=n == EXPERTS - 1)
                    last.then_inc(y_mm, 1)
                    side(n)
                pe.wait_ge(y_sb, k + 1)
                for j in range(4):
                    last = pe.transpose(ps[7][:, 128 * j:128 * j + 128], yT[:, 128 * j:128 * j + 128], ident[:, :])
                last.then_inc(yt_mm, 1)

            pe.wait_ge(side_free, SIDE_USES)
            feed_forward(step, side)


def _half_size(n):
    import numpy as np
    lo, hi = np.zeros((n // 2, n)), np.zeros((n // 2, n))
    for i in range(n // 2):
        lo[i, 2 * i] = lo[i, 2 * i + 1] = hi[i, 2 * i] = 0.7071067811865476
        hi[i, 2 * i + 1] = -0.7071067811865476
    return lo, hi


def _resize(n, m):
    import numpy as np
    at = (np.arange(m) + 0.5) * n / m - 0.5
    w = np.maximum(0.0, 1.0 - np.abs(at[:, None] - np.arange(n)[None]) * m / n)
    return w / w.sum(1, keepdims=True)


def _constants():
    import numpy as np
    lo1, hi1 = _half_size(PX)
    lo2, hi2 = _half_size(PX // 2)
    small, large = _resize(PX // 4, GRID), _resize(PX // 2, GRID)
    ops = [small @ lo2 @ lo1, small @ hi2 @ lo1, large @ lo1, large @ hi1]
    rows = np.concatenate(ops, 0).T
    maps = [(0, 0), (1, 0), (0, 1), (1, 1), (3, 2), (2, 3), (3, 3)]
    cols = np.zeros((PX, 4, FROWS))
    for m, (r, c) in enumerate(maps):
        cols[:, r, m * GRID:(m + 1) * GRID] = ops[c].T
    ident = np.eye(128)
    pick = np.zeros((24, EXPERTS, 128))
    for e in range(EXPERTS):
        pick[e::EXPERTS, e, :] = 1.0
    rev = np.tile(EXPERTS - np.arange(EXPERTS), (128, 1))
    fold = np.tile(np.eye(D), (2, 2))
    mask, one = np.zeros((2, FROWS, GRID)), np.zeros((2, FROWS, 1))
    mask[:, :MAPS * GRID] = np.tile(np.eye(GRID), (MAPS, 1))
    mask[:, MAPS * GRID] = one[:, MAPS * GRID] = 1.0
    mask, one = mask.reshape(128, GRID), one.reshape(128, 1)
    return [np.ascontiguousarray(a, dtype=np.float32) for a in (rows, cols, ident, pick, rev, fold, mask, one)]


_INS = ['x', 'L0_tok_W', 'L0_tok_b', 'L0_attn_Q', 'L0_attn_K', 'L0_attn_VO', 'L0_ffn_gamma', 'L0_ffn_beta', 'L0_ffn_Wr',
        'L0_ffn_br', 'L0_ffn_W1', 'L0_ffn_b1', 'L0_ffn_W2', 'L0_ffn_b2']
_CONST = ['row_ops', 'col_ops', 'ident', 'pick', 'rev', 'fold', 'mask', 'one']


def kernel(**inputs):
    import numpy as _np
    import concourse.bacc as _bacc
    from concourse import mybir as _mybir
    from concourse.bass_utils import run_bass_kernel_spmd as _run

    nc = _bacc.Bacc("TRN2", target_bir_lowering=False, num_devices=1)
    arrays, args = {}, []
    given = [(n, _np.ascontiguousarray(inputs[n])) for n in _INS] + list(zip(_CONST, _constants()))
    for name, a in given:
        arrays[f"in_{name}_dram"] = a
        args.append(nc.dram_tensor(f"in_{name}_dram", a.shape, _mybir.dt.from_np(a.dtype), kind="ExternalInput").ap())
    args.append(nc.dram_tensor("out_dram", (IMGS, T, D), _mybir.dt.float32, kind="ExternalOutput").ap())
    vit_block(nc, *args)
    r = _run(nc, [arrays], core_ids=[0])
    return r.results[0]["out_dram"]
```

```python
import concourse.bass as bass
from concourse import mybir
from contextlib import ExitStack

F32 = mybir.dt.float32
F32R = mybir.dt.float32r
BF16 = mybir.dt.bfloat16
ALU = mybir.AluOpType
ACT = mybir.ActivationFunctionType
AX = mybir.AxisListType

IMGS, PX, T, D = 64, 84, 64, 64
GRID = 8
HEADS, R = 8, 32
EXPERTS, HID = 8, 128
HALVES, PAIRS = 2, 16
NPAIR = HALVES * PAIRS
GP = 4
GCOL = GP * 2 * T
NG = NPAIR // GP
TOK = IMGS * T
MAPS = 7
FROWS = 64
QCOL = 512
NQ = TOK // (2 * QCOL)
EPS = 1e-5
BIG = -3.0e38
MAGIC = 0x5F3759DF
I32 = mybir.dt.int32


BUSY = (3, 16, 6, 2, 3, 3, 5)
X_BANKS = (0, 1, 2, 3, 5, 6, 7, 4)


def vit_block(nc, x, tok_w, tok_b, wq, wk, wvo, gamma, beta, wr, br, w1, b1, w2, b2,
              ops_c, square_c, pick_c, out):
    ctx = ExitStack()
    with ctx:
        def sb(name, shape, dt=F32):
            return ctx.enter_context(nc.sbuf_tensor(name, shape, dt))

        def sem(name):
            return ctx.enter_context(nc.semaphore(name))

        early = sb("early", [128, IMGS * 2 * PX])
        img = early[0:PX // 2, :].rearrange("r (b s w) -> r b s w", b=IMGS, s=2)
        hid = early[:, 0:4 * QCOL].rearrange("p (b c) -> p b c", b=4)
        hw = early[:, 4 * QCOL:8 * QCOL].rearrange("p (b c) -> p b c", b=4)
        yT = early[:, 8 * QCOL:9 * QCOL]
        gq = early[:, 9 * QCOL:17 * QCOL].rearrange("p (b q t) -> p b q t", b=2, q=4)
        xd = early[:, 17 * QCOL:19 * QCOL].rearrange("p (b t) -> p b t", b=2)
        pn = early[:, 19 * QCOL:21 * QCOL].rearrange("p (b t) -> p b t", b=2)
        ops = sb("ops", [PX, 8 * GRID + 4 * FROWS])
        rowop = ops[0:PX // 2, 0:8 * GRID].rearrange("r (s k) -> r s k", s=2)
        colop = ops[:, 8 * GRID:].rearrange("w (r k) -> w r k", r=4)
        t0 = sb("t0", [128, PAIRS, PX])
        t1 = sb("t1", [PX, 16, PAIRS, GRID])
        feat = sb("feat", [128, 2 * PAIRS * GRID])
        square = sb("square", [128, 2 * 128 + 2 * GRID + 1])
        ident = square[:, 0:128]
        fold_f = square[:, 128:256]
        mask = square[:, 256:256 + GRID]
        rev = square[:, 256 + GRID:256 + 2 * GRID]
        one = square[:, 256 + 2 * GRID:]
        wrep = sb("wrep", [128, D])
        wavg = sb("wavg", [128, 1])
        wtok = sb("wtok", [128, GRID, D])
        wmean = sb("wmean", [128, GRID])
        identb = sb("identb", [128, 128], BF16)
        busy = sb("busy", [128, 128], BF16)
        fold = sb("fold", [128, 128], F32R)
        pick_f = sb("pick_f", [24, EXPERTS, 128])
        pick = sb("pick", [24, EXPERTS, 128], BF16)
        h = sb("h", [128, NQ, 2, 4, D])
        xc = sb("xc", [128, NQ, 2, 4, D])
        sq = sb("sq", [128, NQ, 2, 4, D])
        x12 = sb("x12", [128, 8 * NQ, 2, D])
        xT = sb("xT", [128, TOK], F32R)
        xfT = sb("xfT", [128, TOK], F32R)
        mean = sb("mean", [128, 8 * NQ])
        var = sb("var", [128, 8 * NQ])
        hvar = sb("hvar", [128, 8 * NQ])
        rstd = sb("rstd", [128, 8 * NQ])
        tmp = sb("tmp", [128, 8 * NQ])
        gam = sb("gam", [128, 1])
        bet = sb("bet", [128, 1])
        q_s = sb("q_s", [R, HEADS, D])
        k_s = sb("k_s", [R, HEADS, 2, D])
        qk1 = sb("qk1", [128, HEADS * D], F32R)
        qk2 = sb("qk2", [128, HEADS * D], F32R)
        vo = sb("vo", [128, 4, D])
        sc = sb("sc", [128, 2, 512])
        ex = sb("ex", [128, 2, 512])
        pT = sb("pT", [128, 2, 512])
        vv = sb("vv", [128, 2, 2, 4, D])
        mx = sb("mx", [128, 2, HEADS])
        sm = sb("sm", [128, 2, HEADS])
        rs = sb("rs", [128, 2, HEADS])
        oT = sb("oT", [128, NPAIR * T])
        w1_s = sb("w1_s", [128, EXPERTS * HID])
        w1a = sb("w1a", [128, EXPERTS * HID], F32R)
        w1b = sb("w1b", [128, EXPERTS * HID], F32R)
        b1_s = sb("b1_s", [HID, EXPERTS])
        b1f = sb("b1f", [HID, EXPERTS])
        w2_s = sb("w2_s", [HID, EXPERTS, D])
        b2_s = sb("b2_s", [24, D])
        b2r = sb("b2r", [24, D])
        b2p = sb("b2p", [24, 3, D], BF16)
        wr_s = sb("wr_s", [128, EXPERTS])
        wrab = sb("wrab", [128, 2 * EXPERTS], F32R)
        br_s = sb("br_s", [128, EXPERTS])
        brf = sb("brf", [128, EXPERTS])
        lg = sb("lg", [128, 16, EXPERTS])
        lg2 = sb("lg2", [128, 16, EXPERTS])
        oh1 = sb("oh1", [128, 16, EXPERTS])
        oh2 = sb("oh2", [128, 16, EXPERTS])
        ca = sb("ca", [128, 16, EXPERTS])
        lp = sb("lp", [128, 256])
        top1 = sb("top1", [128, 16])
        top2 = sb("top2", [128, 16])
        at = sb("at", [128, 16])
        lead = sb("lead", [128, 2, 16])
        g1 = sb("g1", [128, 16])
        g2 = sb("g2", [128, 16])
        gp = sb("gp", [128, 16, 3, EXPERTS], BF16)
        gT = sb("gT", [24, TOK], BF16)
        gTs = sb("gTs", [24, 2 * QCOL], BF16)
        banks = ctx.enter_context(nc.psum_tensor("banks", [128, 8, 512], F32))
        ps = [banks[:, b, :] for b in range(8)]
        VPB, TB, OB, SIDE = ps[4], ps[5], ps[6], ps[7]
        YB = ps[6]

        ld_x = [sem(f"ld_x{c}") for c in range(4)]
        ld_row, ld_con, ld_tok, ld_att, ld_ffn, ld_ffp = (sem(n) for n in ("ld_row", "ld_con", "ld_tok", "ld_att", "ld_ffn", "ld_ffp"))
        busy_sb, wr_sb, lp_mm, lp_sb = sem("busy_sb"), sem("wr_sb"), sem("lp_mm"), sem("lp_sb")
        zeroed, consts, wtok_sb, wprep, bias_mm, bias_sb = (sem(n) for n in ("zeroed", "consts", "wtok_sb", "wprep", "bias_mm", "bias_sb"))
        t0_mm, t0_act, t0_dve, t1_mm, t1_act, t1_dve = (sem(n) for n in ("t0_mm", "t0_act", "t0_dve", "t1_mm", "t1_act", "t1_dve"))
        ft_mm, ft_sb, mean_mm, h_mm, h_sb = (sem(n) for n in ("ft_mm", "ft_sb", "mean_mm", "h_mm", "h_sb"))
        qk_mm, qk_half, qk_sb = sem("qk_mm"), sem("qk_half"), sem("qk_sb")
        dve_step = sem("dve_step")
        centred, squared, normed, part1, part2 = (sem(n) for n in ("centred", "squared", "normed", "part1", "part2"))
        xt_mm, xt_act, xt_dve = sem("xt_mm"), sem("xt_act"), sem("xt_dve")
        x_mm, x_sb, prep_mm, prep_sb = sem("x_mm"), sem("x_sb"), sem("prep_mm"), sem("prep_sb")
        s_mm, mx_done, s_sub, e_done, sm_done, r_done, p_norm = (sem(n) for n in (
            "s_mm", "mx_done", "s_sub", "e_done", "sm_done", "r_done", "p_norm"))
        t_mm, t_sb, v_mm, v_sb, o_mm, o_sb = (sem(n) for n in ("t_mm", "t_sb", "v_mm", "v_sb", "o_mm", "o_sb"))
        side_mm, side_free = sem("side_mm"), sem("side_free")
        join_mm, join_sb, mean_sb, lg_sb, pool_step = (sem(n) for n in ("join_mm", "join_sb", "mean_sb", "lg_sb", "pool_step"))
        rstd_sb, gates_mm, gates_sb = sem("rstd_sb"), sem("gates_mm"), sem("gates_sb")
        lead_v, lead_t, gate_sp = sem("lead_v"), sem("lead_t"), sem("gate_sp")
        gts_sb, u_mm, g_mm, hid_sb, hw_sb, y_mm, y_sb, yt_mm, h_out, stored = (sem(n) for n in (
            "gts_sb", "u_mm", "g_mm", "hid_sb", "hw_sb", "y_mm", "y_sb", "yt_mm", "h_out", "stored"))
        block = ctx.enter_context(nc.Block())

        def halfs(t, f):
            return t[:, 2 * f:2 * f + 2].rearrange("p k a j e -> p (k a j) e")

        def centre(engine, f, first=0, last=16):
            m = mean[:, 16 * f + first:16 * f + last].unsqueeze(2).to_broadcast([128, last - first, D])
            return engine.tensor_tensor(halfs(xc, f)[:, first:last], halfs(h, f)[:, first:last], m, ALU.subtract)

        def apply(engine, f):
            c = slice(16 * f, 16 * f + 16)
            return engine.tensor_tensor(halfs(sq, f), halfs(xc, f), rstd[:, c].unsqueeze(2).to_broadcast([128, 16, D]), ALU.mult)

        def second_part(engine, f):
            c = slice(16 * f, 16 * f + 16)
            return engine.tensor_tensor(x12[:, c, 1, :], halfs(sq, f), x12[:, c, 0, :], ALU.subtract)

        def gates(engine, link, f):
            up = lambda ap: ap.unsqueeze(2).to_broadcast([128, 16, EXPERTS])
            engine.wait_ge(lead_t, f + 1)
            engine.tensor_scalar(g1[:, :], lead[:, 1, :], 0.5, 0.5, ALU.mult, ALU.add)
            link(engine.tensor_scalar(g2[:, :], lead[:, 1, :], -0.5, 0.5, ALU.mult, ALU.add))
            engine.tensor_tensor(oh1[:, :, :], oh1[:, :, :], up(g1[:, :]), ALU.mult)
            link(engine.tensor_tensor(oh2[:, :, :], oh2[:, :, :], up(g2[:, :]), ALU.mult))
            link(engine.tensor_tensor(oh1[:, :, :], oh1[:, :, :], oh2[:, :, :], ALU.add))

        def gate_parts(engine, link):
            link(engine.tensor_copy(gp[:, :, 0, :], oh1[:, :, :]))
            link(engine.tensor_tensor(oh2[:, :, :], oh1[:, :, :], gp[:, :, 0, :], ALU.subtract))
            link(engine.tensor_copy(gp[:, :, 1, :], oh2[:, :, :]))
            engine.tensor_tensor(gp[:, :, 2, :], oh2[:, :, :], gp[:, :, 1, :], ALU.subtract).then_inc(gate_sp, 1)

        def attention(slot, side):
            with slot.engine.Fori(0, NG // 4) as i:
                for q in range(2):
                    for p in range(GP):
                        slot(i * 2 + q, q, p, i * (2 * GP) + (q * GP + p), 2)
            for g in range(NG // 2, NG):
                for p in range(GP):
                    slot(g, g % 2, p, g * GP + p, min(2, NG - 1 - g))
                    side(0, (g - NG // 2) * GP + p)

        def feed_forward(step, side, before_loop=lambda: None):
            for k in range(NQ // 2):
                step(k, lambda n: side(1, 8 * k + n))
            before_loop()
            with step.engine.Fori(NQ // 2, NQ) as k:
                step(k, lambda n: None)

        def on(engine):
            def mark(f):
                f.engine = engine
                return f
            return mark

        @block.sync
        def _(sp):
            xv = x.rearrange("b c (r s) w -> r (b c) (s w)", s=2)
            for c in range(4):
                for f in range(HALVES):
                    b = 32 * f + 8 * c
                    sp.dma_start(img[:, b:b + 8, :, :].rearrange("r b s w -> r b (s w)"), xv[:, b:b + 8, :]).then_inc(ld_x[c], 16)
            sp.dma_start(w1_s[0:D, :].rearrange("d (n k) -> d n k", k=HID), w1.rearrange("n d k -> d n k")).then_inc(ld_ffn, 16)
            sp.dma_start(w1_s[D:128, :].rearrange("d (n k) -> d n k", k=HID), w1.rearrange("n d k -> d n k")).then_inc(ld_ffn, 16)
            sp.dma_start(w2_s[:, :, :], w2.rearrange("n k d -> k n d")).then_inc(ld_ffn, 16)
            sp.dma_start(pick_f[:, :, :], pick_c).then_inc(ld_ffn, 16)
            ov = out.rearrange("(f m a) (i q j) e -> f q a m i (j e)", f=HALVES, a=2, i=GRID, q=2)
            for k in range(NQ):
                sp.wait_ge(h_out, k + 1)
                for a in range(2):
                    sp.dma_start(ov[k // 2, k % 2, a], h[:, k, a, :, :].rearrange("p j e -> p (j e)")).then_inc(stored, 16)
            sp.wait_ge(stored, 32 * NQ)

        @block.gpsimd
        def _(pool):
            pool.memset(wrep[:, :], 0.0).then_inc(zeroed, 1)
            pool.wait_ge(zeroed, 1)
            for f in range(HALVES):
                pool.dma_start(wrep[64 * f:64 * f + MAPS * GRID, :], tok_w.unsqueeze(1).to_broadcast([MAPS, GRID, D])).then_inc(ld_tok, 16)
                pool.dma_start(wrep[64 * f + MAPS * GRID:64 * f + MAPS * GRID + 1, :], tok_b.rearrange("(a e) -> a e", a=1)).then_inc(ld_tok, 16)
            for f in range(2):
                c = slice(64 * f, 64 * f + 64)
                pool.dma_start(gam[c, :], gamma.rearrange("(e a) -> e a", a=1)).then_inc(ld_ffp, 16)
                pool.dma_start(bet[c, :], beta.rearrange("(e a) -> e a", a=1)).then_inc(ld_ffp, 16)
                pool.dma_start(wr_s[c, :], wr).then_inc(ld_ffp, 16)
            pool.dma_start(br_s[:, :], br.rearrange("(a e) -> a e", a=1).to_broadcast([128, EXPERTS])).then_inc(ld_ffp, 16)
            for c in range(3):
                pool.dma_start(b2_s[8 * c:8 * c + 8, :], b2).then_inc(ld_ffp, 16)
            with nc.allow_non_contiguous_dma(reason="4 KB of biases, hidden unit on partitions"):
                pool.dma_start(b1_s[:, :], b1.rearrange("n k -> k n")).then_inc(ld_ffp, 16)

            steps = [0]

            def link(ins):
                steps[0] += 1
                ins.then_inc(pool_step, 1)
                pool.wait_ge(pool_step, steps[0])

            pool.wait_ge(ld_ffn, 16 * 4)
            pool.tensor_copy(pick[:, :, :], pick_f[:, :, :]).then_inc(wprep, 1)
            pool.wait_ge(ld_ffp, 16 * 11)
            link(pool.tensor_copy(b2p[:, 0, :], b2_s[:, :]))
            link(pool.tensor_tensor(b2r[:, :], b2_s[:, :], b2p[:, 0, :], ALU.subtract))
            link(pool.tensor_copy(b2p[:, 1, :], b2r[:, :]))
            pool.tensor_tensor(b2p[:, 2, :], b2r[:, :], b2p[:, 1, :], ALU.subtract).then_inc(wprep, 1)

            pool.wait_ge(mean_sb, 1)
            pool.wait_ge(h_sb, 2)
            centre(pool, 1).then_inc(centred, 1)

            def norm(n, b):
                pool.wait_ge(r_done, n + 1)
                pool.tensor_tensor(
                    pn[:, b, :].rearrange("p (q o u) -> p o q u", o=2, u=T),
                    ex[:, b, :].rearrange("p (o q u) -> p o q u", o=2, u=T),
                    rs[:, b, :].rearrange("p (o q) -> p o q", o=2).unsqueeze(3).to_broadcast([128, 2, 4, T]),
                    ALU.mult).then_inc(p_norm, 1)

            norm(0, 0)

            @on(pool)
            def slot(g, gb, p, n, left):
                if p < GP - 1 or left >= 1:
                    norm(n + 1, (p + 1) % 2)

            def to_feed_forward(f, step):
                if step == 2:
                    pool.wait_ge(mean_sb, 2 + f)
                    centre(pool, f, 8 * (1 - f)).then_inc(centred, 1)
                if step == 4:
                    pool.wait_ge(rstd_sb, 1 + f)
                    apply(pool, f).then_inc(normed, 1)
                if step == 5:
                    pool.wait_ge(part1, 3 + f)
                    second_part(pool, f).then_inc(part2, 1)

            attention(slot, to_feed_forward)
            for step in (2, 4, 5):
                to_feed_forward(1, step)
            gates(pool, link, 1)
            gate_parts(pool, link)

        @block.scalar
        def _(act):
            act.dma_start(ops[:, :], ops_c).then_inc(ld_row, 16)
            act.dma_start(square[:, :], square_c).then_inc(ld_con, 16)
            act.dma_start(q_s[:, :, :], wq.rearrange("h r d -> r h d")).then_inc(ld_att, 16)
            for c in range(2):
                act.dma_start(k_s[:, :, c, :], wk.rearrange("h r d -> r h d")).then_inc(ld_att, 16)
            for o in range(2):
                act.dma_start(vo[64 * o:64 * o + 64, :, :], wvo.rearrange("(q o) d e -> o d q e", o=2)[o]).then_inc(ld_att, 16)
            for c in (1, 3):
                act.wait_ge(t0_mm, c + 1)
                act.activation(t0[:, 4 * c:4 * c + 4, :].rearrange("p m w -> p (m w)"), ps[c][:, 0:4 * PX], ACT.Copy).then_inc(t0_act, 1)
            for c in (1, 3):
                act.wait_ge(t1_mm, c + 1)
                act.activation(t1[:, :, 4 * c:4 * c + 4, :].rearrange("w r m i -> w m r i"),
                               ps[4 + c][0:PX, :].rearrange("w (m r i) -> w m r i", m=4, i=GRID), ACT.Copy).then_inc(t1_act, 1)
            def residual(f):
                for a in range(2):
                    act.wait_ge(h_mm, 2 * f + a + 1)
                    if f == 0:
                        act.wait_ge(centred, a + 1)
                    act.activation(h[:, 2 * f:2 * f + 2, a, :, :], ps[2 + 2 * f + a][:, :].rearrange("p (q j e) -> p q j e", q=2, e=D),
                                   ACT.Copy).then_inc(h_sb, 1)

            def squares(f, count):
                act.wait_ge(centred, count)
                act.activation(halfs(sq, f), halfs(xc, f), ACT.Square).then_inc(squared, 1)

            def first_part(f, count):
                act.wait_ge(normed, count)
                act.activation(x12[:, 16 * f:16 * f + 16, 0, :].bitcast(F32R), halfs(sq, f), ACT.Copy).then_inc(part1, 1)

            def xt_out(c):
                act.wait_ge(xt_mm, c + 1)
                f, q, a = c // 4, (c // 2) % 2, c % 2
                act.activation(
                    xT[:, :].rearrange("p (f m a j i) -> p f a j m i", f=2, m=PAIRS, a=2, i=GRID)[:, f, a, 4 * q:4 * q + 4],
                    ps[X_BANKS[c]][:, :].rearrange("p (j m i) -> p j m i", j=4, i=GRID), ACT.Copy).then_inc(xt_act, 1)

            squares(0, 2)
            residual(1)
            residual(0)
            act.wait_ge(qk_mm, 1)
            act.activation(qk1[:, :], ps[6][:, :], ACT.Copy, scale=1.0 / 8.0).then_inc(qk_half, 1)
            squares(1, 3)
            first_part(0, 1)
            xt_out(1)
            xt_out(3)

            def x_twice(g, gb):
                act.wait_ge(x_mm, g + 1)
                act.activation(xd[:, gb, :], SIDE[:, :], ACT.Copy).then_inc(x_sb, 1)

            def prep(k, gb, q, bank=VPB):
                act.wait_ge(prep_mm, k + 1)
                act.activation(gq[:, gb, q, :], bank[:, :], ACT.Copy).then_inc(prep_sb, 1)

            def exps(n, b):
                act.wait_ge(s_sub, n + 1)
                act.activation(ex[:, b, :], sc[:, b, :], ACT.Exp).then_inc(e_done, 1)

            def values(n, b):
                act.wait_ge(v_mm, n + 1)
                act.activation(vv[:, b].rearrange("p a q e -> p (a q e)"), VPB[:, :], ACT.Copy).then_inc(v_sb, 1)

            x_twice(0, 0)
            for k in range(6):
                if k == 3:
                    first_part(1, 2)
                prep(k, k // 4, k % 4, (VPB, ps[2])[k % 2])
            exps(0, 0)
            values(0, 0)
            xt_out(5)
            xt_out(7)
            exps(1, 1)

            @on(act)
            def slot(g, gb, p, n, left):
                act.wait_ge(t_mm, n + 1)
                act.activation(pT[:, p % 2, :], TB[:, :], ACT.Copy).then_inc(t_sb, 1)
                if p == 0 and left >= 1:
                    x_twice(g + 1, 1 - gb)
                if p < GP - 1 or left >= 1:
                    values(n + 1, (p + 1) % 2)
                if isinstance(n, int):
                    between(0, n - NPAIR // 2)
                if p < 2 and left >= 1:
                    prep(n + 6, 1 - gb, p + 2)
                if p >= 2 and left >= 2:
                    prep(n + 6, gb, p - 2)
                if p < 2 or left >= 1:
                    exps(n + 2, p % 2)
                if p == GP - 1:
                    act.wait_ge(o_mm, g + 1)
                    act.activation(
                        oT[:, :].rearrange("p (j c) -> p j c", j=GRID)[:, :, bass.ds(g * (GP * GRID), GP * GRID)].rearrange("p j (m i) -> p j m i", i=GRID),
                        OB[:, 0:GP * T].rearrange("p (m j i) -> p j m i", m=GP, j=GRID), ACT.Copy).then_inc(o_sb, 1)

            def input_out(f, c):
                act.wait_ge(side_mm, 5 * f + 1 + c)
                act.activation(xfT[:, f * 2048 + c * 512:f * 2048 + c * 512 + 512], SIDE[:, :], ACT.Copy).then_inc(side_free, 1)

            def lead_out(f):
                act.wait_ge(lead_v, f + 1)
                act.activation(lead[:, 1, :], lead[:, 0, :], ACT.Tanh, scale=0.5).then_inc(lead_t, 1)

            def gates_out(f):
                act.wait_ge(side_mm, 6 * f + 5)
                act.activation(gT[:, f * 2048:f * 2048 + 1024], SIDE[0:24, :].bitcast(BF16), ACT.Copy).then_inc(side_free, 1)

            def side(f, step):
                if step == (2, 1)[f]:
                    squares(f, 5 + f)
                if f == 1 and step == 5:
                    first_part(1, 4)
                first = (6, 7)[f]
                if first <= step < first + 4:
                    input_out(f, step - first)
                if f == 0 and step == 10:
                    act.wait_ge(lp_mm, 1)
                    act.activation(lp[:, :], OB[:, 256:512], ACT.Copy).then_inc(lp_sb, 1)
                if f == 1 and step == 13:
                    lead_out(1)
                if f == 0 and step == 15:
                    units(0, 0)
                if f == 1 and step == 15:
                    gates_out(1)

            def between(f, step):
                if step == 5:
                    first_part(0, 3)
                if step == 13:
                    lead_out(0)
                if step == 15:
                    gates_out(0)

            def units(k, n):
                for a in range(2):
                    b = 2 * (n % 2) + a
                    act.wait_ge(u_mm, k * 16 + (2 * n + a + 1))
                    act.activation(hid[:, b, :], ps[b][:, :], ACT.Gelu, bias=b1f[:, n:n + 1]).then_inc(hid_sb, 1)

            attention(slot, side)

            @on(act)
            def step(k, side):
                for n in range(EXPERTS):
                    if n or not (isinstance(k, int) and k == 0):
                        units(k, n)
                    side(n)
                act.wait_ge(y_mm, k * 8 + 8)
                act.activation(yT[:, :], YB[:, :], ACT.Copy).then_inc(y_sb, 1)

            feed_forward(step, side)

        @block.vector
        def _(dve):
            steps = [0]

            def link(ins):
                steps[0] += 1
                ins.then_inc(dve_step, 1)
                dve.wait_ge(dve_step, steps[0])

            def rsqrt(y, v, half_v, t, first, last):
                if first == 0:
                    dve.tensor_scalar(half_v, v, -0.5, None, ALU.mult)
                    link(dve.tensor_scalar(y.bitcast(I32), v.bitcast(I32), 1, None, ALU.logical_shift_right))
                    link(dve.tensor_scalar(y.bitcast(I32), y.bitcast(I32), -1.0, float(MAGIC), ALU.mult, ALU.add))
                for _ in range(first, last):
                    link(dve.tensor_tensor(t, y, y, ALU.mult))
                    link(dve.tensor_tensor(t, t, half_v, ALU.mult))
                    link(dve.scalar_tensor_tensor(y, t, 1.5, y, op0=ALU.add, op1=ALU.mult))

            def weights(part):
                if part == 0:
                    link(dve.tensor_scalar(w1a[:, :], w1_s[:, :], gam[:, :], None, ALU.mult))
                if part == 1:
                    dve.scalar_tensor_tensor(w1b[:, :], w1_s[:, :], gam[:, :], w1a[:, :].bitcast(F32),
                                             op0=ALU.mult, op1=ALU.subtract).then_inc(wprep, 1)
                if part == 3:
                    link(dve.tensor_scalar(wrab[:, 0:EXPERTS], wr_s[:, :], gam[:, :], None, ALU.mult))
                    dve.scalar_tensor_tensor(wrab[:, EXPERTS:2 * EXPERTS], wr_s[:, :], gam[:, :], wrab[:, 0:EXPERTS].bitcast(F32),
                                             op0=ALU.mult, op1=ALU.subtract).then_inc(wr_sb, 1)
                if part == 2:
                    dve.wait_ge(ld_ffn, 16 * 4)
                    dve.wait_ge(ld_ffp, 16 * 11)
                    dve.wait_ge(bias_mm, 1)
                    dve.tensor_tensor(b1f[:, :], b1_s[:, :], ps[7][:, 128:136], ALU.add).then_inc(bias_sb, 1)
                    dve.tensor_tensor(brf[:, :], br_s[:, :], ps[7][:, 136:144], ALU.add).then_inc(bias_sb, 1)

            dve.memset(busy[:, :], 1.0).then_inc(busy_sb, 1)
            dve.wait_ge(ld_con, 16)
            dve.tensor_copy(identb[:, :], ident[:, :]).then_inc(consts, 1)
            dve.tensor_copy(fold[:, :], fold_f[:, :]).then_inc(consts, 1)
            dve.wait_ge(ld_tok, 64)
            link(dve.reduce_sum(wavg[:, :], wrep[:, :], axis=AX.X))
            link(dve.tensor_scalar(wavg[:, :], wavg[:, :], 1.0 / D, None, ALU.mult))
            dve.tensor_scalar(wmean[:, :], mask[:, :], wavg[:, :], None, ALU.mult).then_inc(wtok_sb, 1)
            dve.tensor_tensor(wtok[:, :, :], wrep[:, :].unsqueeze(1).to_broadcast([128, GRID, D]),
                              mask[:, :].unsqueeze(2).to_broadcast([128, GRID, D]), ALU.mult).then_inc(wtok_sb, 1)
            for c in (0, 2):
                dve.wait_ge(t0_mm, c + 1)
                dve.tensor_copy(t0[:, 4 * c:4 * c + 4, :].rearrange("p m w -> p (m w)"), ps[c][:, 0:4 * PX]).then_inc(t0_dve, 1)
            for c in (0, 2):
                dve.wait_ge(t1_mm, c + 1)
                dve.tensor_copy(t1[:, :, 4 * c:4 * c + 4, :].rearrange("w r m i -> w m r i"),
                                ps[4 + c][0:PX, :].rearrange("w (m r i) -> w m r i", m=4, i=GRID)).then_inc(t1_dve, 1)
            dve.wait_ge(ft_mm, 1)
            dve.tensor_scalar(feat[:, :], ps[0][:, 0:256], one[:, :], None, ALU.add).then_inc(ft_sb, 1)
            dve.wait_ge(mean_mm, 1)
            link(dve.tensor_copy(mean[:, :].rearrange("p (f q a j) -> p f q a j", f=2, q=2, a=2)[:, 0],
                                 ps[0][:, 0:16].rearrange("p (a q j) -> p q a j", a=2, q=2)))
            link(dve.tensor_copy(mean[:, :].rearrange("p (f q a j) -> p f q a j", f=2, q=2, a=2)[:, 1],
                                 ps[6][:, 0:16].rearrange("p (a q j) -> p q a j", a=2, q=2)))
            dve.sem_inc(mean_sb, 1)
            for a in range(2):
                    dve.wait_ge(h_mm, a + 1)
                    for q in range(2):
                        k = q
                        ins = dve.tensor_tensor(
                            xc[:, k, a, :, :], ps[2 + a][:, 256 * q:256 * q + 256].rearrange("p (j e) -> p j e", j=4),
                            mean[:, 8 * k + 4 * a:8 * k + 4 * a + 4].unsqueeze(2).to_broadcast([128, 4, D]), ALU.subtract)
                    ins.then_inc(centred, 1)

            def scale(f, count, one_eps, eps):
                c = slice(16 * f, 16 * f + 16)
                dve.wait_ge(squared, count)
                link(dve.reduce_sum(var[:, c], halfs(sq, f), axis=AX.X))
                link(dve.tensor_scalar(var[:, c], var[:, c], one_eps / D, eps, ALU.mult, ALU.add))

            def newton(f, first=0, last=3):
                c = slice(16 * f, 16 * f + 16)
                rsqrt(rstd[:, c], var[:, c], hvar[:, c], tmp[:, c], first, last)

            def xt_out(c):
                dve.wait_ge(xt_mm, c + 1)
                f, q, a = c // 4, (c // 2) % 2, c % 2
                dve.tensor_copy(
                    xT[:, :].rearrange("p (f m a j i) -> p f a j m i", f=2, m=PAIRS, a=2, i=GRID)[:, f, a, 4 * q:4 * q + 4],
                    ps[X_BANKS[c]][:, :].rearrange("p (j m i) -> p j m i", j=4, i=GRID)).then_inc(xt_dve, 1)

            scale(0, 1, 1.0, EPS)
            newton(0)
            apply(dve, 0).then_inc(normed, 1)
            scale(1, 2, 1.0, EPS)
            dve.wait_ge(part1, 1)
            second_part(dve, 0).then_inc(part2, 1)
            dve.wait_ge(qk_half, 1)
            dve.scalar_tensor_tensor(qk2[:, :], ps[6][:, :], 1.0 / 8.0, qk1[:, :].bitcast(F32),
                                     op0=ALU.mult, op1=ALU.subtract).then_inc(qk_sb, 1)
            xt_out(0)
            xt_out(2)
            weights(2)
            newton(1)
            apply(dve, 1).then_inc(normed, 1)

            def less_max(n, b):
                dve.wait_ge(s_mm, n + 1)
                raw = banks[:, 2 * b:2 * b + 2, 0:256].rearrange("p o (q u) -> p o q u", u=T)
                peak = mx[:, b, :].rearrange("p (o q) -> p o q", o=2)
                dve.reduce_max(peak, raw, axis=AX.X).then_inc(mx_done, 1)
                dve.wait_ge(mx_done, n + 1)
                dve.tensor_tensor(sc[:, b, :].rearrange("p (o q u) -> p o q u", o=2, u=T), raw,
                                  peak.unsqueeze(3).to_broadcast([128, 2, 4, T]), ALU.subtract).then_inc(s_sub, 1)

            def sums(n, b):
                dve.wait_ge(e_done, n + 1)
                dve.reduce_sum(sm[:, b, :], ex[:, b, :].rearrange("p (h u) -> p h u", u=T), axis=AX.X).then_inc(sm_done, 1)
                dve.wait_ge(sm_done, n + 1)
                dve.reciprocal(rs[:, b, :], sm[:, b, :]).then_inc(r_done, 1)

            dve.wait_ge(part1, 2)
            second_part(dve, 1).then_inc(part2, 1)
            less_max(0, 0)
            sums(0, 0)
            xt_out(4)
            xt_out(6)
            less_max(1, 1)

            @on(dve)
            def slot(g, gb, p, n, left):
                if p < GP - 1 or left >= 1:
                    sums(n + 1, (p + 1) % 2)
                if isinstance(n, int):
                    between(n - NPAIR // 2)
                if p < 2 or left >= 1:
                    less_max(n + 2, p % 2)

            def largest(src, onehot, top):
                link(dve.reduce_max(top[:, :], src[:, :, :], axis=AX.X))
                link(dve.tensor_tensor(onehot[:, :, :], src[:, :, :], top[:, :].unsqueeze(2).to_broadcast([128, 16, EXPERTS]), ALU.is_equal))

            def first_of(onehot):
                link(dve.tensor_tensor(ca[:, :, :], onehot[:, :, :], rev[:, :].unsqueeze(1).to_broadcast([128, 16, EXPERTS]), ALU.mult))
                link(dve.reduce_max(at[:, :], ca[:, :, :], axis=AX.X))
                link(dve.tensor_tensor(onehot[:, :, :], ca[:, :, :], at[:, :].unsqueeze(2).to_broadcast([128, 16, EXPERTS]), ALU.is_equal))

            def join(f, q):
                k = 2 * f + q
                bank = SIDE if f == 0 else ps[4 + q]
                dve.wait_ge(join_mm, k + 1)
                hk = h[:, k].rearrange("p a j e -> p j a e")
                dve.tensor_tensor(hk, hk, bank[:, :].rearrange("p (j a e) -> p j a e", j=4, e=D), ALU.add).then_inc(join_sb, 1)

            def means(f):
                c = slice(16 * f, 16 * f + 16)
                dve.wait_ge(join_sb, 2 * f + 2)
                link(dve.reduce_sum(mean[:, c], halfs(h, f), axis=AX.X))
                dve.tensor_scalar(mean[:, c], mean[:, c], 1.0 / D, None, ALU.mult).then_inc(mean_sb, 1)

            def gates_out(f):
                dve.wait_ge(gates_mm, f + 1)
                dve.tensor_copy(gT[:, f * 2048 + 1024:f * 2048 + 2048], SIDE[0:24, :].bitcast(BF16)).then_inc(gates_sb, 1)

            def variance(f):
                scale(f, 3 + f, 1.0 + EPS, EPS * EPS)

            def top_one(f):
                if f == 0:
                    dve.wait_ge(lp_sb, 1)
                else:
                    dve.wait_ge(side_mm, 5 + 5)
                E3 = [128, 16, EXPERTS]
                two = (lp[:, :], SIDE[:, 0:256])[f].rearrange("p (s c n) -> p s c n", c=2, n=EXPERTS)
                link(dve.tensor_tensor(lg[:, :, :], two[:, :, 0, :], brf[:, :].unsqueeze(1).to_broadcast(E3), ALU.add))
                dve.tensor_tensor(lg[:, :, :], lg[:, :, :], two[:, :, 1, :], ALU.add).then_inc(lg_sb, 1)
                dve.wait_ge(lg_sb, f + 1)
                largest(lg, oh1, top1)

            def top_two():
                link(dve.scalar_tensor_tensor(lg2[:, :, :], oh1[:, :, :], BIG, lg[:, :, :], op0=ALU.mult, op1=ALU.add))
                largest(lg2, oh2, top2)

            def lead_of():
                first_of(oh2)
                dve.tensor_tensor(lead[:, 0, :], top1[:, :], top2[:, :], ALU.subtract).then_inc(lead_v, 1)

            def between(step):
                if step == 1:
                    join(0, 1)
                if step == 2:
                    dve.wait_ge(mean_sb, 2)
                    centre(dve, 0, 0, 8).then_inc(centred, 1)
                if step == 3:
                    variance(0)
                if step == 4:
                    newton(0, 1, 3)
                    dve.sem_inc(rstd_sb, 1)
                if step == 7:
                    weights(0)
                if step == 11:
                    top_one(0)
                if step == 12:
                    top_two()
                if step == 14:
                    gate_parts(dve, link)

            def side(f, step):
                if f == 0:
                    if step == 0:
                        join(0, 0)
                    if step == 1:
                        means(0)
                    if step == 3:
                        newton(0, 0, 1)
                    if step == 6:
                        weights(3)
                    if step == 8:
                        weights(1)
                    if step == 11:
                        first_of(oh1)
                    if step == 12:
                        lead_of()
                    if step == 13:
                        gates(dve, link, 0)
                else:
                    if step == 1:
                        variance(1)
                    if step == 2:
                        newton(1, 0, 1)
                    if step == 3:
                        newton(1, 1, 3)
                        dve.sem_inc(rstd_sb, 1)
                    if step == 5:
                        gates_out(0)
                    if step == 11:
                        top_one(1)
                        first_of(oh1)
                    if step == 12:
                        top_two()
                        lead_of()

            attention(slot, side)

            def result(k, done):
                dve.wait_ge(yt_mm, done)
                hk = h[:, :, :, :, :].rearrange("p k a j e -> p (k a j e)")[:, bass.ds(k * 512, 512)].rearrange(
                    "p (a j e) -> p j a e", a=2, e=D)
                dve.tensor_tensor(hk, hk, ps[7][:, :].rearrange("p (j a e) -> p j a e", j=4, e=D), ALU.add).then_inc(h_out, 1)

            def stage(k):
                dve.tensor_copy(gTs[:, :], gT[:, bass.ds(k * (2 * QCOL), 2 * QCOL)]).then_inc(gts_sb, 1)

            dve.wait_ge(side_free, 5)
            stage(0)
            join(1, 0)
            join(1, 1)
            means(1)

            @on(dve)
            def step(k, side):
                if not (isinstance(k, int) and k == 0):
                    dve.wait_ge(y_mm, k * 8)
                    if isinstance(k, int):
                        dve.wait_ge(gates_sb, 1)
                    stage(k)
                for n in range(EXPERTS):
                    for a in range(2):
                        b = 2 * (n % 2) + a
                        dve.wait_ge(hid_sb, k * 16 + (2 * n + a + 1))
                        dve.wait_ge(g_mm, k * 16 + (2 * n + a + 1))
                        if n >= 2:
                            dve.wait_ge(y_mm, k * 8 + (n - 1))
                        dve.tensor_tensor(hw[:, b, :], hid[:, b, :], ps[4 + a][:, :], ALU.mult).then_inc(hw_sb, 1)
                    if n == 0 and not (isinstance(k, int) and k == 0):
                        result(k - 1, k)
                    side(n)

            def second_gates():
                gates_out(1)
                dve.wait_ge(side_free, 10)
                dve.wait_ge(gates_sb, 2)

            feed_forward(step, side, second_gates)
            result(NQ - 1, NQ)

        @block.tensor
        def _(pe):
            def keep_busy(count, bank=ps[7]):
                for _ in range(count):
                    pe.matmul(bank[:, :], busy[:, :], busy[:, :].unsqueeze(1).to_broadcast([128, 4, 128]), start=True, stop=True)

            pe.wait_ge(busy_sb, 1)
            pe.wait_ge(ld_row, 16)
            for c in range(4):
                pe.wait_ge(ld_x[c], 32)
                for r in range(2):
                    for q in range(4):
                        b = 32 * (q // 2) + 8 * c + q % 2
                        last = pe.matmul(banks[32 * q:32 * q + 32, c, 0:4 * PX], rowop[:, r, :], img[:, b:b + 7:2, r, :],
                                         start=r == 0, stop=r == 1)
                last.then_inc(t0_mm, 1)
            pe.wait_ge(ld_con, 16)
            for c in range(4):
                pe.wait_ge((t0_dve, t0_act)[c % 2], c // 2 + 1)
                for m in range(4):
                    last = pe.transpose(ps[4 + c][0:PX, 128 * m:128 * m + 128], t0[:, 4 * c + m, :], ident[:, :])
                last.then_inc(t1_mm, 1)
            pe.wait_ge(t1_act, 2)
            pe.wait_ge(t1_dve, 2)
            tv = t1[:, :, :, :].rearrange("w (f a r) m i -> w f a r (m i)", f=2, a=2)
            for r in range(4):
                for f in range(HALVES):
                    last = pe.matmul(ps[0][64 * f:64 * f + 64, 0:256], colop[:, r, :], tv[:, f, :, r, :], start=r == 0, stop=r == 3)
            last.then_inc(ft_mm, 1)
            keep_busy(BUSY[0])
            pe.wait_ge(ft_sb, 1)
            pe.wait_ge(wtok_sb, 2)
            for m in range(4):
                f, a = m // 2, m % 2
                last = pe.matmul(ps[6 * f][:, 8 * a:8 * a + 8], feat[64 * f:64 * f + 64, 128 * a:128 * a + 128],
                                 wmean[64 * f:64 * f + 64, :], start=True, stop=True)
            last.then_inc(mean_mm, 1)
            for m in range(4):
                f, a = m // 2, m % 2
                pe.matmul(ps[2 + m][:, :], feat[64 * f:64 * f + 64, 128 * a:128 * a + 128],
                          wtok[64 * f:64 * f + 64, :, :].rearrange("k j e -> k (j e)"), start=True, stop=True).then_inc(h_mm, 1)
            pe.wait_ge(ld_att, 80)
            pe.wait_ge(mean_sb, 1)
            for hd in range(HEADS):
                last = pe.matmul(ps[6][:, hd * D:(hd + 1) * D], k_s[:, hd, :, :], q_s[:, hd, :], start=True, stop=True)
            last.then_inc(qk_mm, 1)
            keep_busy(BUSY[1])
            pe.wait_ge(ld_ffn, 16 * 4)
            pe.wait_ge(ld_ffp, 16 * 11)
            for n in range(EXPERTS):
                pe.matmul(ps[7][:, 128 + n:129 + n], w1_s[0:D, n * HID:(n + 1) * HID], bet[0:D, :], start=True, stop=True)
            pe.matmul(ps[7][:, 136:144], bet[0:D, :].to_broadcast([D, 128]), wr_s[0:D, :], start=True, stop=True).then_inc(bias_mm, 1)
            def x_turned(c):
                bank = ps[X_BANKS[c]]
                for j in range(4):
                    last = pe.transpose(bank[:, 128 * j:128 * j + 128], x12[:, 4 * c + j, :, :].rearrange("p a e -> p (a e)"), ident[:, :])
                last.then_inc(xt_mm, 1)

            pe.wait_ge(h_sb, 4)
            pe.wait_ge(part2, 1)
            for c in range(4):
                x_turned(c)
            pe.wait_ge(consts, 2)
            pe.wait_ge(qk_sb, 1)
            pe.wait_ge(xt_act, 2)
            pe.wait_ge(xt_dve, 2)

            def x_twice(g):
                pe.matmul(SIDE[:, :], fold[:, :], xT[:, bass.ds(g * GCOL, GCOL)], start=True, stop=True).then_inc(x_mm, 1)

            def prep(g, q, bank=VPB):
                cols = xT[:, bass.ds(g * GCOL, GCOL)]
                w = slice(128 * q, 128 * q + 128)
                pe.matmul(bank[:, :], qk1[:, w], cols, start=True, stop=False)
                pe.matmul(bank[:, :], qk2[:, w], cols, start=False, stop=True).then_inc(prep_mm, 1)

            def scores(n, gb, p, b):
                for o, a in ((0, 0), (1, 1), (1, 0), (0, 1)):
                    t0 = 128 * p + 64 * a
                    last = pe.matmul(banks[64 * a:64 * a + 64, 2 * b + o, 0:256], xd[64 * o:64 * o + 64, gb, t0:t0 + 64],
                                     gq[64 * o:64 * o + 64, gb, :, t0:t0 + 64], start=True, stop=True)
                last.then_inc(s_mm, 1)

            def values(n, gb, p):
                for a in range(2):
                    for o in range(2):
                        t0 = 128 * p + 64 * a
                        last = pe.matmul(VPB[64 * o:64 * o + 64, 256 * a:256 * a + 256], xd[64 * o:64 * o + 64, gb, t0:t0 + 64],
                                         vo[64 * o:64 * o + 64, :, :].rearrange("p q e -> p (q e)"), start=True, stop=True)
                last.then_inc(v_mm, 1)

            pe.wait_ge(bias_sb, 2)
            x_twice(0)
            for k in range(6):
                if k == 5:
                    keep_busy(BUSY[2], ps[5])
                if k >= 2:
                    pe.wait_ge(prep_sb, k - 1)
                prep(k // 4, k % 4, (VPB, ps[2])[k % 2])
            pe.wait_ge(x_sb, 1)
            scores(0, 0, 0, 0)
            pe.wait_ge(prep_sb, 6)
            scores(1, 0, 1, 1)
            values(0, 0, 0)
            pe.wait_ge(part2, 2)
            for c in range(4, 8):
                if c == 7:
                    pe.wait_ge(v_sb, 1)
                x_turned(c)
            pe.wait_ge(xt_dve, 4)
            pe.wait_ge(xt_act, 4)

            @on(pe)
            def slot(g, gb, p, n, left):
                total = NPAIR
                if isinstance(n, int):
                    pe.wait_ge(prep_sb, min(n + 6, total))
                else:
                    pe.wait_ge(prep_sb, n + 6)
                if p == 2 and left >= 1:
                    pe.wait_ge(x_sb, g + 2)
                pe.wait_ge(v_sb, n + 1)
                pe.wait_ge(p_norm, n + 1)
                for q in range(4):
                    last = pe.transpose(TB[:, 128 * q:128 * q + 128], pn[:, p % 2, 128 * q:128 * q + 128], ident[:, :])
                last.then_inc(t_mm, 1)
                if isinstance(n, int) and n == NPAIR // 2 + 1:
                    outputs(0, 1)
                if isinstance(n, int) and n == NPAIR - 1:
                    gates_turned(0, 0)
                if p == 0 and left >= 1:
                    if isinstance(n, int) and n > NPAIR // 2:
                        pe.wait_ge(join_sb, 2)
                        if n - NPAIR // 2 == 8:
                            pe.wait_ge(side_free, 2)
                    x_twice(g + 1)
                if p < GP - 1:
                    values(n + 1, gb, p + 1)
                elif left >= 1:
                    values(n + 1, 1 - gb, 0)
                if p < 2:
                    scores(n + 2, gb, p + 2, p % 2)
                elif left >= 1:
                    scores(n + 2, 1 - gb, p - 2, p % 2)
                if (p < 2 and left >= 1) or left >= 2:
                    pe.wait_ge(v_sb, n + 2)
                    prep(g + 1 if p < 2 else g + 2, (p + 2) % 4)
                if isinstance(n, int) and 7 <= n - NPAIR // 2 < 11:
                    c = n - NPAIR // 2 - 7
                    logits(0, 4 * c, 4 * c + 4)
                pe.wait_ge(t_sb, n + 1)
                for q in range(4):
                    for a in range(2):
                        last = pe.matmul(OB[64 * a:64 * a + 64, T * p:T * p + T], vv[:, p % 2, a, q, :],
                                         pT[:, p % 2, 128 * q + 64 * a:128 * q + 64 * a + 64], start=q == 0, stop=q == 3)
                if p == GP - 1:
                    last.then_inc(o_mm, 1)
                if isinstance(n, int) and n - NPAIR // 2 == 10:
                    last.then_inc(lp_mm, 1)

            def outputs(f, q):
                if f == 0 and q == 0:
                    pe.wait_ge(x_sb, NG // 2 + 2)
                if q == 0:
                    pe.wait_ge(o_sb, 4 * f + 4)
                if f == 0 and q == 1:
                    pe.wait_ge(join_sb, 1)
                bank = SIDE if f == 0 else ps[4 + q]
                for j in range(4):
                    c = 256 * (4 * q + j) + 128 * f
                    last = pe.transpose(bank[:, 128 * j:128 * j + 128], oT[:, c:c + 128], ident[:, :])
                last.then_inc(join_mm, 1)

            def gates_turned(f, c):
                if c == 0:
                    pe.wait_ge(gate_sp, f + 1)
                    pe.wait_ge(lg_sb, f + 1)
                else:
                    pe.wait_ge(side_free, 5 * f + 5)
                for s in range(8):
                    last = pe.transpose(SIDE[0:24, :].bitcast(BF16)[:, 128 * s:128 * s + 128],
                                        gp[:, 8 * c + s, :, :].rearrange("p c n -> p (c n)"), identb[:, :])
                last.then_inc((side_mm, gates_mm)[c], 1)

            def input_turned(f, c):
                if c == 0:
                    pe.wait_ge(part2, 3 + f)
                    if f == 1:
                        pe.wait_ge(gates_sb, 1)
                if f == 0 and c == 2:
                    pe.wait_ge(x_sb, NG)
                if f == 1 and c == 2:
                    pe.wait_ge(h_out, 1)
                if 5 * f + c:
                    pe.wait_ge(side_free, 5 * f + c)
                for j in range(4):
                    last = pe.transpose(SIDE[:, 128 * j:128 * j + 128],
                                        x12[:, 16 * f + 4 * c + j, :, :].rearrange("p a e -> p (a e)"), ident[:, :])
                last.then_inc(side_mm, 1)

            def logits(f, first, last):
                bank = OB[:, 256:512] if f == 0 else SIDE[:, 0:256]
                if first == 0:
                    pe.wait_ge(wr_sb, 1)
                pe.wait_ge(side_free, 9 if f else last // 4)
                for s in range(first, last):
                    t = f * 2048 + 128 * s
                    ins = pe.matmul(bank[:, 16 * s:16 * s + 16], xfT[:, t:t + 128], wrab[:, :], start=True, stop=True)
                if f == 1:
                    ins.then_inc(side_mm, 1)

            def hidden(k, n):
                for a in range(2):
                    b = 2 * (n % 2) + a
                    if n >= 2:
                        pe.wait_ge(hid_sb, k * 16 + (2 * (n - 2) + a + 1))
                    cols = xfT[:, bass.ds(k * (2 * QCOL) + a * QCOL, QCOL)]
                    pe.matmul(ps[b][:, :], w1a[:, n * HID:(n + 1) * HID], cols, start=True, stop=False)
                    pe.matmul(ps[b][:, :], w1b[:, n * HID:(n + 1) * HID], cols, start=False, stop=True).then_inc(u_mm, 1)

            def side(f, step):
                if f == 0 and step == 0:
                    outputs(0, 0)
                if 6 <= step < 10:
                    input_turned(f, step - 6)
                if f == 1 and step == 10:
                    logits(1, 0, 16)
                if f == 0 and 11 <= step < 14:
                    keep_busy(BUSY[3 + step - 11], SIDE)
                if f == 0 and step == 14:
                    pe.wait_ge(wprep, 3)
                if f == 0 and step >= 14:
                    hidden(0, step - 14)
                if f == 1 and step == 4:
                    gates_turned(0, 1)
                if f == 1 and step == 14:
                    gates_turned(1, 0)

            attention(slot, side)

            @on(pe)
            def step(k, side):
                def spread(n):
                    for a in range(2):
                        if n >= 1:
                            pe.wait_ge(hw_sb, k * 16 + (2 * (n - 1) + a + 1))
                        pe.matmul(ps[4 + a][:, :], pick[:, n, :], gTs[:, a * QCOL:(a + 1) * QCOL], start=True, stop=True).then_inc(g_mm, 1)

                first = isinstance(k, int) and k == 0
                if not first:
                    hidden(k, 0)
                pe.wait_ge(gts_sb, k + 1)
                if first:
                    pe.wait_ge(join_sb, 4)
                spread(0)
                if not first:
                    hidden(k, 1)
                    turned(k)
                for c in range(3):
                    for a in range(2):
                        pe.matmul(YB[64 * a:64 * a + 64, :], b2p[:, c, :], gTs[:, a * QCOL:(a + 1) * QCOL],
                                  start=c == 0, stop=False)
                if first:
                    pe.wait_ge(side_free, 5)
                    keep_busy(BUSY[6], SIDE)
                for n in range(EXPERTS):
                    if 0 < n < EXPERTS - 1:
                        hidden(k, n + 1)
                    if n + 1 < EXPERTS:
                        spread(n + 1)
                    pe.wait_ge(hw_sb, k * 16 + (2 * n + 2))
                    for a in range(2):
                        last = pe.matmul(YB[64 * a:64 * a + 64, :], w2_s[:, n, :], hw[:, 2 * (n % 2) + a, :],
                                         start=False, stop=n == EXPERTS - 1)
                    last.then_inc(y_mm, 1)
                    side(n)

            def turned(done):
                pe.wait_ge(y_sb, done)
                if isinstance(done, int) and done == 1:
                    pe.wait_ge(side_free, 7)
                for j in range(4):
                    last = pe.transpose(ps[7][:, 128 * j:128 * j + 128], yT[:, 128 * j:128 * j + 128], ident[:, :])
                last.then_inc(yt_mm, 1)

            outputs(1, 0)
            outputs(1, 1)

            feed_forward(step, side, lambda: gates_turned(1, 1))
            turned(NQ)


def _half_size(n):
    import numpy as np
    lo, hi = np.zeros((n // 2, n)), np.zeros((n // 2, n))
    for i in range(n // 2):
        lo[i, 2 * i] = lo[i, 2 * i + 1] = hi[i, 2 * i] = 0.7071067811865476
        hi[i, 2 * i + 1] = -0.7071067811865476
    return lo, hi


def _resize(n, m):
    import numpy as np
    at = (np.arange(m) + 0.5) * n / m - 0.5
    w = np.maximum(0.0, 1.0 - np.abs(at[:, None] - np.arange(n)[None]) * m / n)
    return w / w.sum(1, keepdims=True)


def _constants():
    import numpy as np
    lo1, hi1 = _half_size(PX)
    lo2, hi2 = _half_size(PX // 2)
    small, large = _resize(PX // 4, GRID), _resize(PX // 2, GRID)
    ops = [small @ lo2 @ lo1, small @ hi2 @ lo1, large @ lo1, large @ hi1]
    rows = np.concatenate(ops, 0).T
    maps = [(0, 0), (1, 0), (0, 1), (1, 1), (3, 2), (2, 3), (3, 3)]
    cols = np.zeros((PX, 4, FROWS))
    for m, (r, c) in enumerate(maps):
        cols[:, r, m * GRID:(m + 1) * GRID] = ops[c].T
    ident = np.eye(128)
    pick = np.zeros((24, EXPERTS, 128))
    for e in range(EXPERTS):
        pick[e::EXPERTS, e, :] = 1.0
    rev = np.tile(EXPERTS - np.arange(EXPERTS), (128, 1))
    fold = np.tile(np.eye(D), (2, 2))
    mask, one = np.zeros((2, FROWS, GRID)), np.zeros((2, FROWS, 1))
    mask[:, :MAPS * GRID] = np.tile(np.eye(GRID), (MAPS, 1))
    mask[:, MAPS * GRID] = one[:, MAPS * GRID] = 1.0
    mask, one = mask.reshape(128, GRID), one.reshape(128, 1)
    pairs = np.zeros((PX, 8 * GRID))
    pairs[:PX // 2] = rows.reshape(PX // 2, 8 * GRID)
    ops = np.concatenate([pairs, cols.reshape(PX, 4 * FROWS)], 1)
    square = np.concatenate([ident, fold, mask, rev, one], 1)
    return [np.ascontiguousarray(a, dtype=np.float32) for a in (ops, square, pick)]


_INS = ['x', 'L0_tok_W', 'L0_tok_b', 'L0_attn_Q', 'L0_attn_K', 'L0_attn_VO', 'L0_ffn_gamma', 'L0_ffn_beta', 'L0_ffn_Wr',
        'L0_ffn_br', 'L0_ffn_W1', 'L0_ffn_b1', 'L0_ffn_W2', 'L0_ffn_b2']
_CONST = ['ops', 'square', 'pick']


def kernel(**inputs):
    import numpy as _np
    import concourse.bacc as _bacc
    from concourse import mybir as _mybir
    from concourse.bass_utils import run_bass_kernel_spmd as _run

    nc = _bacc.Bacc("TRN2", target_bir_lowering=False, num_devices=1)
    arrays, args = {}, []
    given = [(n, _np.ascontiguousarray(inputs[n])) for n in _INS] + list(zip(_CONST, _constants()))
    for name, a in given:
        arrays[f"in_{name}_dram"] = a
        args.append(nc.dram_tensor(f"in_{name}_dram", a.shape, _mybir.dt.from_np(a.dtype), kind="ExternalInput").ap())
    args.append(nc.dram_tensor("out_dram", (IMGS, T, D), _mybir.dt.float32, kind="ExternalOutput").ap())
    vit_block(nc, *args)
    r = _run(nc, [arrays], core_ids=[0])
    return r.results[0]["out_dram"]
```
